# Optimizing a Trainium2 kernel written in Bass

```python
import numpy as np
import jax
import jax.numpy as jnp

def _softmax(x, axis=-1):
    return jax.nn.softmax(x, axis=axis)

def _gelu(x):
    return jax.nn.gelu(x, approximate=True)

def _silu(x):
    return jax.nn.silu(x)

def _sigmoid(x):
    return jax.nn.sigmoid(x)

def _layernorm(x, axis=-1, eps=1e-05):
    m = jnp.mean(x, axis=axis, keepdims=True)
    v = jnp.var(x, axis=axis, keepdims=True)
    return (x - m) / jnp.sqrt(v + eps)

def _scatter_add(tgt, idx, src, axis=0):
    return tgt.at[idx].add(src)

def _segment_sum(src, seg, n):
    return jax.ops.segment_sum(src, seg, n)
kernel_name = 'mk_early_fusion_d1_tok_img4096_r4_9fc80b'

def setup_inputs(seed: int=0):
    np.random.seed(seed)
    _w = jnp.asarray

    def _rec_inputs():
        import jax
        import jax.numpy as jnp
        _rk = jax.random.key(seed)
        x = -0.0064186 + 0.999588 * jax.random.normal(jax.random.fold_in(_rk, 1), (64, 128, 64, 2), jnp.float32)
        txt = 0.000163725 + 0.02 * jax.random.normal(jax.random.fold_in(_rk, 2), (64, 77, 1024), jnp.float32)
        return (x, txt)
    x, txt = _rec_inputs()

    def _L0_tok_setup():
        import jax, jax.numpy as jnp
        import numpy as np
        import math
        H, N, C, L_VAL = (128, 64, 1, 1024)
        EPS = 1e-07

        def _reciprocal(x, epsilon):
            xc = jnp.conj(x)
            return xc / (x * xc + epsilon)
        key = jax.random.key(seed)
        k1, k2, k3 = jax.random.split(key, 3)
        log_dt = math.log(0.001) + jax.random.uniform(k1, (H,), dtype=jnp.float32) * (math.log(0.1) - math.log(0.001))
        log_dt = jnp.tile(log_dt[:, None], (1, 2))
        lam_im = jax.random.normal(k2, (N,), dtype=jnp.float32)
        Lambda = jnp.stack([-0.5 * jnp.ones((N,), jnp.float32), lam_im], axis=-1)
        W = jax.random.normal(k3, (C, H, N, 2), dtype=jnp.float32)
        return {'log_dt': log_dt, 'Lambda': Lambda, 'W': W, 'L': L_VAL}
    _L0_tok_all = _L0_tok_setup()
    _L0_tok_in = {k: v for k, v in _L0_tok_all.items() if k in ('log_dt', 'Lambda')}
    del _L0_tok_all

    def _L0_attn_setup():
        import jax, jax.numpy as jnp
        import numpy as np
        import math
        D_MODEL = 512
        D_STATE = 16
        EXPAND = 2
        D_INNER = D_MODEL * EXPAND
        DT_RANK = math.ceil(D_MODEL / 16)
        BATCH, SEQ_LEN = (2, 128)
        key = jax.random.key(seed)
        ks = jax.random.split(key, 6)
        x = jax.random.normal(ks[0], (BATCH, SEQ_LEN, D_INNER), dtype=jnp.float32)
        A_log = jnp.log(jax.random.uniform(ks[1], (D_INNER, D_STATE), minval=0.5, maxval=16.0, dtype=jnp.float32))
        D = jnp.ones((D_INNER,), dtype=jnp.float32)
        x_proj_w = 0.02 * jax.random.normal(ks[2], (DT_RANK + 2 * D_STATE, D_INNER), dtype=jnp.float32)
        dt_init_std = DT_RANK ** (-0.5)
        dt_proj_w = jax.random.uniform(ks[3], (D_INNER, DT_RANK), minval=-dt_init_std, maxval=dt_init_std, dtype=jnp.float32)
        dt = jnp.exp(jax.random.uniform(ks[4], (D_INNER,), dtype=jnp.float32) * (math.log(0.1) - math.log(0.001)) + math.log(0.001))
        dt = jnp.clip(dt, 0.0001, None)
        dt_proj_b = dt + jnp.log(-jnp.expm1(-dt))
        return {'x': x, 'A_log': A_log, 'D': D, 'x_proj_w': x_proj_w, 'dt_proj_w': dt_proj_w, 'dt_proj_b': dt_proj_b}
    _L0_attn_all = _L0_attn_setup()
    _L0_attn_in = {k: v for k, v in _L0_attn_all.items() if k in ('A_log', 'D', 'x_proj_w', 'dt_proj_w', 'dt_proj_b')}
    del _L0_attn_all

    def _L0_ffn_setup():
        import jax, jax.numpy as jnp
        import numpy as np
        B_L, B_H = (4, 8)
        LIN_SLOPE, LIN_INTER, EST_T = (1.0, 0.0, 64.0)
        BATCH, SEQ, IN_F, OUT_F = (4, 512, 1024, 1024)
        MAX_BITS = 8

        def dequant_kbit(qweight, lut, bit):
            O, I32 = (qweight.shape[1], qweight.shape[2])
            shifts = jnp.arange(32, dtype=jnp.int32)
            idx = jnp.zeros((O, I32 * 32), dtype=jnp.int32)
            for p in range(bit):
                bits = (qweight[p][:, :, None] >> shifts & 1).reshape(O, I32 * 32)
                idx = idx | bits << p
            return jnp.take_along_axis(lut, idx, axis=1)
        key = jax.random.key(seed)
        k = jax.random.split(key, 5)
        x = jax.random.normal(k[0], (BATCH, SEQ, IN_F), dtype=jnp.float32)
        qweight = jax.random.randint(k[1], (MAX_BITS, OUT_F, IN_F // 32), 0, 2147483647, dtype=jnp.int32)
        lut4 = jax.random.normal(k[2], (OUT_F, 2 ** B_L), dtype=jnp.float32) * 0.02
        lut8 = jax.random.normal(k[3], (OUT_F, 2 ** B_H), dtype=jnp.float32) * 0.02
        bias = jax.random.normal(k[4], (OUT_F,), dtype=jnp.float32) * 0.01
        return {'x': x, 'qweight': qweight, 'lut4': lut4, 'lut8': lut8, 'bias': bias}
    _L0_ffn_all = _L0_ffn_setup()
    _L0_ffn_in = {k: v for k, v in _L0_ffn_all.items() if k in ('qweight', 'lut4', 'lut8', 'bias')}
    del _L0_ffn_all
    return {'x': x, 'txt': txt, 'L0_tok_log_dt': _L0_tok_in['log_dt'], 'L0_tok_Lambda': _L0_tok_in['Lambda'], 'L0_attn_A_log': _L0_attn_in['A_log'], 'L0_attn_D': _L0_attn_in['D'], 'L0_attn_x_proj_w': _L0_attn_in['x_proj_w'], 'L0_attn_dt_proj_w': _L0_attn_in['dt_proj_w'], 'L0_attn_dt_proj_b': _L0_attn_in['dt_proj_b'], 'L0_ffn_qweight': _L0_ffn_in['qweight'], 'L0_ffn_lut4': _L0_ffn_in['lut4'], 'L0_ffn_lut8': _L0_ffn_in['lut8'], 'L0_ffn_bias': _L0_ffn_in['bias']}

def reference(x, txt, L0_tok_log_dt, L0_tok_Lambda, L0_attn_A_log, L0_attn_D, L0_attn_x_proj_w, L0_attn_dt_proj_w, L0_attn_dt_proj_b, L0_ffn_qweight, L0_ffn_lut4, L0_ffn_lut8, L0_ffn_bias):
    import jax
    import jax.numpy as jnp

    def _L0_tok_ref(log_dt, Lambda, W, L):
        import jax, jax.numpy as jnp
        import numpy as np
        import math
        H, N, C, L_VAL = (128, 64, 1, 1024)
        EPS = 1e-07

        def _reciprocal(x, epsilon):
            xc = jnp.conj(x)
            return xc / (x * xc + epsilon)
        Lam = Lambda[:, 0] + 1j * Lambda[:, 1]
        Wc = W[..., 0] + 1j * W[..., 1]
        dt = jnp.exp(log_dt)
        dt_Lambda = dt[:, None, 0] * Lambda[None, :, 0] + 1j * (dt[:, None, 1] * Lambda[None, :, 1])
        pos = jnp.arange(L, dtype=jnp.float32)
        gt0 = (Lam.real > 0).astype(dt_Lambda.real.dtype)
        P_max = jax.lax.stop_gradient(dt_Lambda * (gt0 * (L - 1)))
        dt_Lambda_neg = dt_Lambda * (1 - 2 * gt0)
        num = jnp.exp(dt_Lambda_neg) - 1
        den = jnp.exp(dt_Lambda_neg * L) - 1
        Wc = Wc * num * _reciprocal(den * Lam, EPS)
        P = dt_Lambda[..., None] * pos - P_max[..., None]
        K = jnp.einsum('chn,hnl->chl', Wc, jnp.exp(P))
        return K.real.astype(jnp.float32)

    def _L0_attn_ref(x, A_log, D, x_proj_w, dt_proj_w, dt_proj_b):
        import jax, jax.numpy as jnp
        import numpy as np
        import math
        D_MODEL = 512
        D_STATE = 16
        EXPAND = 2
        D_INNER = D_MODEL * EXPAND
        DT_RANK = math.ceil(D_MODEL / 16)
        BATCH, SEQ_LEN = (2, 128)
        A = -jnp.exp(A_log)
        xp = jnp.einsum('bld,rd->blr', x, x_proj_w)
        dt_in = xp[..., :DT_RANK]
        B = xp[..., DT_RANK:DT_RANK + D_STATE]
        C = xp[..., DT_RANK + D_STATE:]
        dt = jax.nn.softplus(jnp.einsum('blr,dr->bld', dt_in, dt_proj_w) + dt_proj_b)
        dA = jnp.exp(dt[..., None] * A)
        dBx = dt[..., None] * B[:, :, None, :] * x[..., None]

        def step(h, inp):
            dA_t, dBx_t, C_t = inp
            h = dA_t * h + dBx_t
            y = jnp.einsum('bdn,bn->bd', h, C_t)
            return (h, y)
        h0 = jnp.zeros((x.shape[0], D_INNER, D_STATE), dtype=x.dtype)
        _, ys = jax.lax.scan(step, h0, (jnp.moveaxis(dA, 1, 0), jnp.moveaxis(dBx, 1, 0), jnp.moveaxis(C, 1, 0)))
        y = jnp.moveaxis(ys, 0, 1) + D * x
        return y

    def _L0_ffn_ref(x, qweight, lut4, lut8, bias):
        import jax, jax.numpy as jnp
        import numpy as np
        B_L, B_H = (4, 8)
        LIN_SLOPE, LIN_INTER, EST_T = (1.0, 0.0, 64.0)
        BATCH, SEQ, IN_F, OUT_F = (4, 512, 1024, 1024)
        MAX_BITS = 8

        def dequant_kbit(qweight, lut, bit):
            O, I32 = (qweight.shape[1], qweight.shape[2])
            shifts = jnp.arange(32, dtype=jnp.int32)
            idx = jnp.zeros((O, I32 * 32), dtype=jnp.int32)
            for p in range(bit):
                bits = (qweight[p][:, :, None] >> shifts & 1).reshape(O, I32 * 32)
                idx = idx | bits << p
            return jnp.take_along_axis(lut, idx, axis=1)
        e = jnp.linalg.norm(x, axis=-1) * LIN_SLOPE + LIN_INTER
        mask = e > EST_T
        w_l = dequant_kbit(qweight, lut4, B_L)
        w_h = dequant_kbit(qweight, lut8, B_H)
        y_l = jnp.einsum('bsi,oi->bso', x, w_l)
        y_h = jnp.einsum('bsi,oi->bso', x, w_h)
        y = jnp.where(mask[..., None], y_h, y_l) + bias
        return y
    h = _L0_tok_ref(L0_tok_log_dt, L0_tok_Lambda, x, 1024)
    h = jnp.concatenate([h, txt], axis=1)
    h = h + _L0_attn_ref(_layernorm(h, axis=-1), L0_attn_A_log, L0_attn_D, L0_attn_x_proj_w, L0_attn_dt_proj_w, L0_attn_dt_proj_b)
    h = h + _L0_ffn_ref(_layernorm(h, axis=-1), L0_ffn_qweight, L0_ffn_lut4, L0_ffn_lut8, L0_ffn_bias)
    return h

_drawn_inputs = setup_inputs


def setup_inputs(seed=0):
    import zlib

    import numpy as np

    out = dict(_drawn_inputs(seed))
    spreads = {'L0_attn_D': (1.0, 0.2)}
    factors = {'L0_ffn_bias': 6.863}
    for name, (base, spread) in spreads.items():
        noise = np.random.default_rng([zlib.crc32(name.encode()), seed]).standard_normal(out[name].shape)
        drawn = base * np.exp(spread * noise) if base else spread * noise
        out[name] = jnp.asarray(drawn.astype(out[name].dtype))
    for name, factor in factors.items():
        out[name] = (out[name] * factor).astype(out[name].dtype)
    return out
```

```python
import math
from contextlib import ExitStack

import concourse.bass as bass
from concourse import mybir

F32 = mybir.dt.float32
BF16 = mybir.dt.bfloat16
I32 = mybir.dt.int32
ALU = mybir.AluOpType
ACT = mybir.ActivationFunctionType

P = 128
BATCH, HEADS, MODES, LK = 64, 128, 64, 1024
TXT = 77
LEN = HEADS + TXT
DIM = 1024
ND = DIM // P
NS = 16
RANK = 32
HALF = LK // 2
EPS_TOK, EPS_LN = 1e-7, 1e-5
ROUND = 1.5 * 2.0 ** 23
INV_TURN = 1.0 / (2.0 * math.pi)
TURN = 6.283185
RESET_DT = 1e37
A_MOST = -1e-30
NORM_LIMIT = 64.0

HG = 8
NG = HEADS // HG
CN = 4
CW = CN * LEN
CHUNKS = ND * NS // CN
LN_EXP_TABLES = 6


def wait(engine, sem, value):
    if isinstance(value, int) and value <= 0:
        return
    engine.wait_ge(sem, value)


def link(engine, sem, counter, instruction):
    counter[0] += 1
    instruction.then_inc(sem, 1)
    engine.wait_ge(sem, counter[0])


def constants(nc, t, dram):
    with ExitStack() as ctx:
        sb = lambda n, s, d=F32: ctx.enter_context(nc.sbuf_tensor(n, s, d))
        sem = lambda n: ctx.enter_context(nc.semaphore(n))
        zero = sb("c_zero", [P, P])
        wide = sb("c_wide", [P, 8])
        row = sb("c_row", [P, 1], I32)
        row15 = sb("c_row15", [P, 1], I32)
        col = sb("c_col", [P, HALF], I32)
        xpw = sb("c_xpw", [2 * RANK, DIM])
        dtw = sb("c_dtw", [P, ND, RANK])
        lut = sb("c_lut", [P, P])
        vec = sb("c_vec", [3 * ND, P])
        ps = [ctx.enter_context(nc.psum_tensor(f"c_ps{i}", [P, 512], F32)) for i in range(4)]
        loaded, alog_in = sem("c_loaded"), sem("c_alog_in")
        pool_step, dve_step, built = sem("c_pool_step"), sem("c_dve_step"), sem("c_built")
        exp_done = sem("c_exp_done")
        turned, copied = sem("c_turned"), sem("c_copied")
        block = ctx.enter_context(nc.Block())

        @block.sync
        def _(sp):
            sp.dma_start(t["a_neg"][:, :, :], dram["A_log"].rearrange("(j p) n -> p j n", p=P)).then_inc(alog_in, 16)
            sp.dma_start(xpw[:, :], dram["x_proj_w"]).then_inc(loaded, 16)
            sp.dma_start(dtw[:, :, :], dram["dt_proj_w"].rearrange("(j p) r -> p j r", p=P)).then_inc(loaded, 16)
            sp.dma_start(lut[:, :], dram["lut4"].rearrange("(g o) b -> g (o b)", o=8)).then_inc(loaded, 16)
            for k, src in enumerate(("D", "dt_proj_b", "bias")):
                sp.dma_start(vec[ND * k:ND * k + ND, :], dram[src].rearrange("(j p) -> j p", p=P)).then_inc(loaded, 16)
            sp.wait_ge(loaded, 16 * 6)

        @block.gpsimd
        def _(pool):
            n = [0]
            link(pool, pool_step, n, nc.gpsimd.memset(zero[:, :], 0.0))
            link(pool, pool_step, n, nc.gpsimd.affine_select(
                out=t["ident"][:, :], in_=zero[:, :], compare_op=ALU.not_equal, fill=1.0, base=0,
                pattern=[[-1, P]], channel_multiplier=1))
            link(pool, pool_step, n, nc.gpsimd.memset(wide[:, :], 1.0))
            link(pool, pool_step, n, nc.gpsimd.affine_select(
                out=wide[:, :], in_=wide[:, :], compare_op=ALU.is_ge, fill=0.0, base=0,
                pattern=[[-16, 8]], channel_multiplier=1))
            link(pool, pool_step, n, nc.gpsimd.affine_select(
                out=t["sel8"][:, :], in_=wide[:, :], compare_op=ALU.is_ge, fill=0.0, base=15,
                pattern=[[16, 8]], channel_multiplier=-1))
            nc.gpsimd.iota(row[:, :], pattern=[[0, 1]], base=0, channel_multiplier=1).then_inc(built, 1)
            nc.gpsimd.iota(col[:, :], pattern=[[1, HALF]], base=0, channel_multiplier=0).then_inc(built, 1)

        @block.scalar
        def _(act):
            act.wait_ge(alog_in, 16)
            nc.scalar.activation(t["a_neg"][:, :, :], t["a_neg"][:, :, :], ACT.Exp).then_inc(exp_done, 1)

        @block.tensor
        def _(pe):
            pe.wait_ge(built, 2)
            pe.wait_ge(loaded, 16 * 6)
            ident = t["ident"]
            for j in range(ND):
                last = nc.tensor.transpose(ps[0][:, 64 * j:64 * j + 64], xpw[:, P * j:P * j + P], ident[0:64, 0:64])
            last.then_inc(turned, 1)
            for j in range(ND):
                last = nc.tensor.transpose(ps[1 + j // 4][0:RANK, P * (j % 4):P * (j % 4) + P], dtw[:, j, :], ident[:, :])
            last.then_inc(turned, 1)
            nc.tensor.transpose(ps[3][:, 0:P], lut[:, :], ident[:, :])
            nc.tensor.transpose(ps[3][:, P:P + 3 * ND], vec[:, :], ident[0:3 * ND, 0:3 * ND]).then_inc(turned, 1)

        @block.vector
        def _(dve):
            n = [0]
            dve.wait_ge(built, 2)
            ident = t["ident"]
            link(dve, dve_step, n, nc.vector.tensor_scalar(row15[:, :], row[:, :], 15, None, ALU.bitwise_and))
            link(dve, dve_step, n, nc.vector.tensor_copy(t["code_col"][:, :], row15[:, :]))
            link(dve, dve_step, n, nc.vector.tensor_copy(t["ramp"][:, :], col[:, :]))
            for c0 in range(0, P, 32):
                link(dve, dve_step, n, nc.vector.tensor_copy(
                    t["spread"][:, 16 * c0:16 * (c0 + 32)].rearrange("p (c b) -> p c b", b=16),
                    ident[:, c0:c0 + 32].unsqueeze(2).broadcast_to([P, 32, 16])))
            for buf in ("mv1", "mv2"):
                link(dve, dve_step, n, nc.vector.memset(t[buf][:, :, :], 1.0))
            link(dve, dve_step, n, nc.vector.memset(t["over"][:, :], 0.0))
            dve.wait_ge(exp_done, 1)
            link(dve, dve_step, n, nc.vector.tensor_scalar(
                t["a_neg"][:, :, :], t["a_neg"][:, :, :], -1.0, A_MOST, ALU.mult, ALU.min))
            dve.wait_ge(turned, 3)
            xt = ps[0][:, :].rearrange("p (j r) -> p j r", j=ND)
            link(dve, dve_step, n, nc.vector.tensor_copy(t["xpw_t"][:, :, :], xt))
            for k in range(2):
                link(dve, dve_step, n, nc.vector.tensor_copy(t["dtw_t"][:, 512 * k:512 * k + 512], ps[1 + k][0:RANK, :]))
            link(dve, dve_step, n, nc.vector.tensor_copy(t["lut_t"][:, :], ps[3][:, 0:P]))
            for k, name in enumerate(("d_col", "dt_bias", "y_bias")):
                link(dve, dve_step, n, nc.vector.tensor_copy(t[name][:, :], ps[3][:, P + ND * k:P + ND * k + ND]))


def token_mixer(nc, t, dram, mixed):
    x = dram["x"].rearrange("c h n r -> c h (n r)")
    with ExitStack() as ctx:
        sb = lambda n, s, d=F32: ctx.enter_context(nc.sbuf_tensor(n, s, d))
        sem = lambda n: ctx.enter_context(nc.semaphore(n))
        pb = lambda n: ctx.enter_context(nc.psum_tensor(n, [P, 512], F32))
        ldt = sb("t_ldt", [P, 2 * HEADS])
        dt = sb("t_dt", [P, 2 * HEADS])
        lam = sb("t_lam", [P, 2])
        growing = sb("t_growing", [P, 1])
        sgn = sb("t_sgn", [P, 1])
        at = sb("t_at", [P, 4])
        role = sb("t_role", [P, 2])
        pos = sb("t_pos", [P, HALF])
        rate = sb("t_rate", [P, HEADS])
        freq = sb("t_freq", [P, HEADS])
        turns = sb("t_turns", [P, HEADS])
        ea = sb("t_ea", [P, 4, HEADS])
        aa = sb("t_aa", [P, 4, HEADS])
        yy = sb("t_yy", [P, 2, 4, HEADS])
        kk = sb("t_kk", [P, 2, 4, HEADS])
        re = sb("t_re", [P, 4, HEADS])
        im = sb("t_im", [P, 4, HEADS])
        w = [sb(f"t_w{i}", [P, HEADS]) for i in range(10)]
        gre = sb("t_gre", [P, 2, HEADS])
        gim = sb("t_gim", [P, 2, HEADS])
        xg = sb("t_xg", [BATCH, 2, HG * 128])
        xs = sb("t_xs", [BATCH, 2, 2, HG, 2, MODES])
        mm1 = sb("t_mm1", [P, 2, HG, BATCH])
        mm2 = sb("t_mm2", [P, 2, HG, BATCH])
        gw = sb("t_gw", [P, 2, HG, 2, BATCH])
        ang = sb("t_ang", [P, HG * HALF])
        near = sb("t_near", [P, HG * HALF])
        mag = sb("t_mag", [P, 2, HG * HALF])
        osc = sb("t_osc", [P, HG * HALF])
        res = sb("t_res", [P, 2, HG, HALF])
        wa, wb = pb("t_wa"), pb("t_wb")
        kb = [pb(f"t_kb{i}") for i in range(4)]
        loaded, dve_step = sem("t_loaded"), sem("t_dve_step")
        dt_exp, arg_ready, arg_done = sem("t_dt_exp"), sem("t_arg_ready"), sem("t_arg_done")
        params = sem("t_params")
        x_in = [sem(f"t_x_in{i}") for i in range(2)]
        swapped, w_turned, w_read, scaled = sem("t_swapped"), sem("t_w_turned"), sem("t_w_read"), sem("t_scaled")
        turned, rounded, reduced = sem("t_turned"), sem("t_rounded"), sem("t_reduced")
        g_half = sem("t_g_half")
        mag_done, sine_done, table = sem("t_mag_done"), sem("t_sine_done"), sem("t_table")
        full = [sem(f"t_full{i}") for i in range(4)]
        empty = [sem(f"t_empty{i}") for i in range(4)]
        out_done = [sem(f"t_out_done{i}") for i in range(2)]
        block = ctx.enter_context(nc.Block())

        def loop(engine, step, tail=None):
            for G in range(4):
                step(G, G % 2, G == 0)
            with engine.Fori(2, NG // 2) as i:
                step(i * 2, 0, False)
                step(i * 2 + 1, 1, False)
            if tail:
                tail(NG - 1, (NG - 1) % 2)

        def out_count(G, half):
            return 16 * (G - half)

        @block.sync
        def _(sp):
            sp.dma_start(ldt[:, :], dram["log_dt"].rearrange("h r -> (h r)").unsqueeze(0).broadcast_to([P, 2 * HEADS])).then_inc(loaded, 16)
            for k in range(2):
                sp.dma_start(lam[64 * k:64 * k + 64, :], dram["Lambda"]).then_inc(loaded, 16)

            def load(G, half, i):
                wait(sp, swapped, G - 1)
                sp.dma_start(xg[:, half, :].rearrange("c (h m) -> c h m", h=HG), x[:, bass.ds(G * HG, HG), :]).then_inc(x_in[half], 16)

            def store(G, half, i):
                for b in range(4):
                    wait(sp, empty[b], 2 * G + 2)
                for a in range(2):
                    sp.dma_start(mixed[:, bass.ds(G * HG, HG), a * HALF:(a + 1) * HALF],
                                 res[64 * a:64 * a + 64, half, :, :]).then_inc(out_done[half], 16)

            load(0, 0, 0)
            load(1, 1, 0)
            with sp.Fori(1, NG // 2) as i:
                load(i * 2, 0, i)
                store(i * 2 - 2, 0, i)
                load(i * 2 + 1, 1, i)
                store(i * 2 - 1, 1, i)
            store(NG - 2, 0, 0)
            store(NG - 1, 1, 0)
            for half in range(2):
                sp.wait_ge(out_done[half], 32 * (NG // 2))

        @block.scalar
        def _(act):
            act.wait_ge(loaded, 48)
            nc.scalar.activation(dt[:, :], ldt[:, :], ACT.Exp).then_inc(dt_exp, 1)
            act.wait_ge(arg_ready, 1)
            nc.scalar.activation(ea[:, :, :], ea[:, :, :], ACT.Exp).then_inc(arg_done, 1)
            nc.scalar.activation(yy[:, :, :, :], yy[:, :, :, :], ACT.Sin, scale=TURN).then_inc(arg_done, 1)
            act.wait_ge(params, 1)

            def evacuate(G, half):
                wait(act, out_done[half], out_count(G, half))
                for h in range(0, HG, 2):
                    b = h % 4
                    act.wait_ge(full[b], 2 * G + h // 4 + 1)
                    nc.scalar.activation(res[:, half, h, :], kb[b][:, :], ACT.Copy).then_inc(empty[b], 1)

            def step(G, half, first):
                wait(act, full[3], 2 * (G - 1))
                for h in range(HG):
                    last = nc.scalar.activation(mag[:, half, h * HALF:(h + 1) * HALF], pos[:, :], ACT.Exp,
                                                scale=rate[:, bass.ds(G * HG + h, 1)])
                last.then_inc(mag_done, 1)
                wait(act, table, HG * G)
                act.wait_ge(reduced, G + 1)
                nc.scalar.activation(osc[:, :], ang[:, :], ACT.Sin, scale=TURN).then_inc(sine_done, 1)
                if not first:
                    evacuate(G - 1, 1 - half)

            loop(act, step, evacuate)

        @block.gpsimd
        def _(pool):
            def step(G, half, first):
                pool.wait_ge(sine_done, G + 1)
                pool.wait_ge(mag_done, G + 1)
                for h in range(HG):
                    s = slice(h * HALF, (h + 1) * HALF)
                    nc.gpsimd.tensor_tensor(mag[:, half, s], mag[:, half, s], osc[:, s], ALU.mult).then_inc(table, 1)
            loop(pool, step)

        @block.vector
        def _(dve):
            n = [0]
            L = lambda ins: link(dve, dve_step, n, ins)
            V = nc.vector
            for r in range(2):
                L(V.memset(role[64 * r:64 * r + 64, 0:1], 1.0 - 2.0 * r))
                L(V.memset(role[64 * r:64 * r + 64, 1:2], 0.25 * (1 - r)))
            dve.wait_ge(loaded, 48)
            L(V.tensor_scalar(growing[:, :], lam[:, 0:1], 0.0, None, ALU.is_gt))
            L(V.tensor_scalar(sgn[:, :], growing[:, :], -2.0, 1.0, ALU.mult, ALU.add))
            L(V.tensor_scalar(at[:, 0:1], sgn[:, :], 1.0, None, ALU.mult))
            L(V.tensor_scalar(at[:, 1:2], sgn[:, :], float(LK), None, ALU.mult))
            L(V.tensor_scalar(at[:, 2:3], growing[:, :], -float(HALF), None, ALU.mult))
            L(V.tensor_scalar(at[:, 3:4], growing[:, :], -float(HALF), float(HALF), ALU.mult, ALU.add))
            L(V.tensor_scalar(w[0][:, 0:1], growing[:, :], float(HALF - 1), None, ALU.mult))
            L(V.tensor_scalar(pos[:, :], t["ramp"][:, :], w[0][:, 0:1], None, ALU.subtract))
            dve.wait_ge(dt_exp, 1)
            d2 = dt[:, :].rearrange("p (h r) -> p r h", r=2)
            L(V.tensor_scalar(rate[:, :], d2[:, 0, :], lam[:, 0:1], None, ALU.mult))
            L(V.tensor_scalar(freq[:, :], d2[:, 1, :], lam[:, 1:2], None, ALU.mult))
            L(V.tensor_scalar(turns[:, :], freq[:, :], INV_TURN, None, ALU.mult))
            for k in range(4):
                L(V.tensor_scalar(ea[:, k, :], rate[:, :], at[:, k:k + 1], None, ALU.mult))
                L(V.tensor_scalar(aa[:, k, :], freq[:, :], at[:, k:k + 1], None, ALU.mult))
            for r, quarter in ((0, 0.25), (1, 0.0)):
                L(V.tensor_scalar(yy[:, r, :, :], aa[:, :, :], INV_TURN, quarter, ALU.mult, ALU.add))
            L(V.tensor_scalar(kk[:, :, :, :], yy[:, :, :, :], ROUND, ROUND, ALU.add, ALU.subtract))
            V.tensor_tensor(yy[:, :, :, :], yy[:, :, :, :], kk[:, :, :, :], ALU.subtract).then_inc(arg_ready, 1)
            dve.wait_ge(arg_done, 2)
            L(V.tensor_tensor(re[:, :, :], ea[:, :, :], yy[:, 0, :, :], ALU.mult))
            L(V.tensor_tensor(im[:, :, :], ea[:, :, :], yy[:, 1, :, :], ALU.mult))
            nr, dr, yr, yi, mg, rr, ri, qr, qi, tmp = (z[:, :] for z in w)
            lre, lim = lam[:, 0:1], lam[:, 1:2]
            ni, di = im[:, 0, :], im[:, 1, :]
            L(V.tensor_scalar(nr, re[:, 0, :], -1.0, None, ALU.add))
            L(V.tensor_scalar(dr, re[:, 1, :], -1.0, None, ALU.add))
            L(V.tensor_scalar(tmp, di, lim, None, ALU.mult))
            L(V.scalar_tensor_tensor(yr, dr, lre, tmp, ALU.mult, ALU.subtract))
            L(V.tensor_scalar(tmp, di, lre, None, ALU.mult))
            L(V.scalar_tensor_tensor(yi, dr, lim, tmp, ALU.mult, ALU.add))
            L(V.tensor_tensor(mg, yr, yr, ALU.mult))
            L(V.tensor_tensor(tmp, yi, yi, ALU.mult))
            L(V.scalar_tensor_tensor(mg, mg, EPS_TOK, tmp, ALU.add, ALU.add))
            L(V.reciprocal(mg, mg))
            L(V.tensor_tensor(rr, yr, mg, ALU.mult))
            L(V.scalar_tensor_tensor(ri, yi, -1.0, mg, ALU.mult, ALU.mult))
            L(V.tensor_tensor(qr, nr, rr, ALU.mult))
            L(V.tensor_tensor(tmp, ni, ri, ALU.mult))
            L(V.tensor_tensor(qr, qr, tmp, ALU.subtract))
            L(V.tensor_tensor(qi, nr, ri, ALU.mult))
            L(V.tensor_tensor(tmp, ni, rr, ALU.mult))
            L(V.tensor_tensor(qi, qi, tmp, ALU.add))
            for a in range(2):
                fr, fi = re[:, 2 + a, :], im[:, 2 + a, :]
                L(V.tensor_tensor(mg, qr, fr, ALU.mult))
                L(V.tensor_tensor(tmp, qi, fi, ALU.mult))
                L(V.tensor_tensor(mg, mg, tmp, ALU.subtract))
                L(V.tensor_scalar(gre[:, a, :], mg, role[:, 0:1], None, ALU.mult))
                L(V.tensor_tensor(mg, qr, fi, ALU.mult))
                L(V.tensor_tensor(tmp, qi, fr, ALU.mult))
                L(V.tensor_tensor(mg, mg, tmp, ALU.add))
                last = V.tensor_scalar(gim[:, a, :], mg, -1.0, None, ALU.mult)
                if a == 0:
                    L(last)
                else:
                    last.then_inc(params, 1)
            dve.wait_ge(params, 1)

            def evacuate(G, half):
                wait(dve, out_done[half], out_count(G, half))
                for h in range(1, HG, 2):
                    b = h % 4
                    dve.wait_ge(full[b], 2 * G + h // 4 + 1)
                    V.tensor_copy(res[:, half, h, :], kb[b][:, :]).then_inc(empty[b], 1)

            def step(G, half, first):
                wait(dve, w_turned, G - 1)
                dve.wait_ge(x_in[half], (G - half) * 8 + 16)
                src = xg[:, half, :].rearrange("c (h n r) -> c h n r", h=HG, r=2)
                for order in range(2):
                    for r in range(2):
                        last = V.tensor_scalar(xs[:, half, order, :, r, :], src[:, :, :, r ^ order], 1.0, None, ALU.mult)
                last.then_inc(swapped, 1)
                wait(dve, sine_done, G)
                for h in range(HG):
                    last = V.tensor_scalar(ang[:, h * HALF:(h + 1) * HALF], pos[:, :], turns[:, bass.ds(G * HG + h, 1)],
                                           role[:, 1:2], ALU.mult, ALU.add)
                last.then_inc(turned, 1)
                dve.wait_ge(turned, G + 1)
                V.tensor_scalar(near[:, :], ang[:, :], ROUND, ROUND, ALU.add, ALU.subtract).then_inc(rounded, 1)
                dve.wait_ge(rounded, G + 1)
                V.tensor_tensor(ang[:, :], ang[:, :], near[:, :], ALU.subtract).then_inc(reduced, 1)
                dve.wait_ge(w_turned, G + 1)
                wait(dve, full[3], 2 * (G - 1))
                va = wa[:, :].rearrange("p (h c) -> p h c", h=HG)
                vb = wb[:, :].rearrange("p (h c) -> p h c", h=HG)
                for a in range(2):
                    ga = gre[:, a, bass.ds(G * HG, HG)].unsqueeze(2).broadcast_to([P, HG, BATCH])
                    gb = gim[:, a, bass.ds(G * HG, HG)].unsqueeze(2).broadcast_to([P, HG, BATCH])
                    V.tensor_tensor(mm1[:, a, :, :], va, ga, ALU.mult)
                    last = V.tensor_tensor(mm2[:, a, :, :], vb, gb, ALU.mult)
                last.then_inc(w_read, 1)
                dve.wait_ge(w_read, G + 1)
                for a in range(2):
                    last = V.tensor_tensor(gw[:, half, :, a, :], mm1[:, a, :, :], mm2[:, a, :, :], ALU.add)
                last.then_inc(scaled, 1)
                dve.wait_ge(scaled, G + 1)
                if not first:
                    evacuate(G - 1, 1 - half)

            loop(dve, step, evacuate)

        @block.tensor
        def _(pe):
            ident = t["ident"]

            def products(G, half):
                for h in range(HG):
                    b = h % 4
                    if h == 0:
                        pe.wait_ge(scaled, G + 1)
                    pe.wait_ge(table, HG * G + h + 1)
                    wait(pe, empty[b], 2 * G + h // 4)
                    nc.tensor.matmul(kb[b][:, :], gw[:, half, h, :, :], mag[:, half, h * HALF:(h + 1) * HALF],
                                     start=True, stop=True).then_inc(full[b], 1)

            def step(G, half, first):
                pe.wait_ge(swapped, G + 1)
                wait(pe, w_read, G)
                for order, bank in ((0, wa), (1, wb)):
                    for h in range(HG):
                        last = nc.tensor.matmul(bank[:, h * BATCH:(h + 1) * BATCH],
                                                xs[:, half, order, h, :, :].rearrange("c r n -> c (r n)"),
                                                ident[0:BATCH, 0:BATCH], start=True, stop=True)
                last.then_inc(w_turned, 1)
                if not first:
                    products(G - 1, 1 - half)

            loop(pe, step, products)


def weight_codes(nc, dve, step, n, qw, part, word, wide, codes, planes):
    V = nc.vector
    U32 = mybir.dt.uint32
    for r in range(4):
        for k, plane in enumerate(planes):
            left = r < k
            link(dve, step, n, V.tensor_scalar(
                part[:, k, :].bitcast(U32), qw[:, plane, :, :].rearrange("p t w -> p (t w)").bitcast(U32), abs(r - k), 0x11111111 << k,
                ALU.logical_shift_left if left else ALU.logical_shift_right, ALU.bitwise_and))
        link(dve, step, n, V.tensor_tensor(part[:, 0:2, :], part[:, 0:2, :], part[:, 2:4, :], ALU.bitwise_or))
        link(dve, step, n, V.tensor_tensor(word[:, r, :], part[:, 0, :], part[:, 1, :], ALU.bitwise_or))
    for r in range(4):
        for j in range(8):
            last = V.tensor_scalar(wide[:, :, 4 * j + r].bitcast(U32), word[:, r, :].bitcast(U32), 4 * j, 15,
                                   ALU.logical_shift_right, ALU.bitwise_and)
    link(dve, step, n, last)
    link(dve, step, n, V.tensor_copy(codes[:, :], wide[:, :, :].rearrange("p a k -> p (a k)")))


def dense_weights(nc, t, dram):
    with ExitStack() as ctx:
        sb = lambda n, s, d=F32: ctx.enter_context(nc.sbuf_tensor(n, s, d))
        sem = lambda n: ctx.enter_context(nc.semaphore(n))
        qw = sb("q_qw", [P, 8, ND, 32], I32)
        part = sb("q_part", [P, 4, 256], I32)
        word = sb("q_word", [P, 4, 256], I32)
        wide = sb("q_wide", [P, 256, 32], I32)
        codes = sb("q_codes", [P, 256 * 32], BF16)
        hot = sb("q_hot", [P, 2, DIM])
        rep = [ctx.enter_context(nc.psum_tensor(f"q_rep{i}", [P, DIM], F32)) for i in range(2)]
        wp = [ctx.enter_context(nc.psum_tensor(f"q_wp{i}", [P, 512], F32)) for i in range(2)]
        loaded, dve_step, coded = sem("q_loaded"), sem("q_dve_step"), sem("q_coded")
        repeated, valued, summed, stored = sem("q_repeated"), sem("q_valued"), sem("q_summed"), sem("q_stored")
        block = ctx.enter_context(nc.Block())

        def over_tiles(engine, tile):
            tile(0)
            with engine.Fori(1, ND) as o:
                tile(o)

        @block.sync
        def _(sp):
            sp.dma_start(qw[:, :, :, :], dram["qweight"].rearrange("b (t p) w -> p b t w", p=P)).then_inc(loaded, 16)
            sp.wait_ge(loaded, 16)

        @block.vector
        def _(dve):
            n = [0]
            V = nc.vector
            dve.wait_ge(loaded, 16)
            weight_codes(nc, dve, dve_step, n, qw, part, word, wide, codes, range(4))
            V.memset(part[:, 0, 0:1], 0).then_inc(coded, 1)

            def store(g8, o, half):
                wait(dve, summed, g8 * 8 + 8)
                V.tensor_scalar(t["w_low"][:, :, bass.ds(o * P + half * 64, 64)],
                                wp[half][:, :].rearrange("p (i c) -> p i c", i=ND), 1.0, None, ALU.mult).then_inc(stored, 1)

            def tile(o):
                for j in range(16):
                    g = o * 16 + j
                    wait(dve, repeated, g + 1)
                    wait(dve, summed, g - 1)
                    V.tensor_scalar(hot[:, j % 2, :], rep[j % 2][:, :], t["code_col"][:, 0:1], t["lut_t"][:, bass.ds(g, 1)],
                                    ALU.is_equal, ALU.mult).then_inc(valued, 1)
                    if j == 8:
                        store(o * 2, o, 0)
                store(o * 2 + 1, o, 1)

            over_tiles(dve, tile)

        @block.tensor
        def _(pe):
            pe.wait_ge(coded, 1)

            def repeat(o, j):
                wait(pe, valued, o * 16 + j - 1)
                for half in range(2):
                    last = nc.tensor.matmul(rep[j % 2][:, 512 * half:512 * half + 512], t["spread"][:, P * j:P * j + P],
                                            codes[:, bass.ds(o * DIM + 512 * half, 512)], start=True, stop=True)
                last.then_inc(repeated, 1)

            def total(o, j):
                wait(pe, valued, o * 16 + j + 1)
                if j % 8 == 0:
                    wait(pe, stored, o * 2 + j // 8 - 1)
                for i in range(ND):
                    c = 64 * i + 8 * (j % 8)
                    last = nc.tensor.matmul(wp[j // 8][:, c:c + 8], hot[:, j % 2, P * i:P * i + P], t["sel8"][:, :],
                                            start=True, stop=True)
                last.then_inc(summed, 1)

            def tile(o):
                for j in range(16):
                    repeat(o, j)
                    if j:
                        total(o, j - 1)
                total(o, 15)

            over_tiles(pe, tile)


X_ADD, X_TURN2, X_TURN1, X_XPROJ, X_DT, X_OUT = 0, 4, 8, 12, 13, 18
X_USES = 22
DT_BLOCKS = (range(0, 2), range(2, 4), range(4, 6), range(6, 7), range(7, 8))

PE_PLAN = {1: [("add", 0)], 2: [("add", 1)], 3: [("add", 2)], 4: [("add", 3)],
           9: [("turn2", 0), ("turn2", 1)], 10: [("turn2", 2), ("turn2", 3)],
           11: [("ffn", (0, 0, 4))], 12: [("ffn", (0, 4, 8))],
           13: [("ffn", (1, 0, 4)), ("turn1", 0)], 14: [("turn1", 1), ("turn1", 2), ("ffn", (1, 4, 8))],
           15: [("turn1", 3), ("ffn", (2, 0, 3))],
           16: [("xproj", (0, 3)), ("ffn", (2, 3, 5))], 17: [("xproj", (3, 6)), ("ffn", (2, 5, 7))],
           18: [("xproj", (6, 8)), ("ffn", (2, 7, 8))],
           19: [("dt", 0), ("ffn", (3, 0, 3))], 20: [("dt", 1), ("ffn", (3, 3, 6))],
           21: [("dt", 2), ("ffn", (3, 6, 8))], 22: [("ffn", (4, 0, 4)), ("dt", 3), ("dt", 4)],
           23: [("ffn", (4, 4, 8))], 24: [("ffn", (5, 0, 4)), ("out", 0)], 25: [("ffn", (5, 4, 8)), ("out", 1)],
           26: [("ffn", (6, 0, 4))], 27: [("ffn", (6, 4, 8))], 28: [("ffn", (7, 0, 4))], 29: [("ffn", (7, 4, 8))],
           30: [("out", 2)], 31: [("out", 3)]}
ACT_PLAN = {5: [("root2", 0)], 7: [("norm2", 0)], 8: [("norm2", 1)],
            10: [("turn2", 0), ("turn2", 1), ("root1", 0)], 11: [("turn2", 2), ("turn2", 3)],
            12: [("norm1", 0)], 13: [("norm1", 1), ("ffn", 0)],
            14: [("turn1", 0)], 15: [("turn1", 1), ("ffn", 1), ("turn1", 2)], 16: [("turn1", 3)],
            19: [("xproj", 0), ("ffn", 2)], 20: [("dt", 0)], 21: [("dt", 1)], 22: [("dt", 2), ("ffn", 3)],
            23: [("dt", 3), ("dt", 4)], 24: [("ffn", 4), ("soft", (0, 0))], 25: [("soft", (0, 1))],
            26: [("ffn", 5), ("soft", (0, 2))], 27: [("soft", (1, 0))], 28: [("ffn", 6), ("soft", (1, 1))],
            29: [("soft", (1, 2))], 30: [("ffn", 7)]}
DVE_PLAN = {2: [("add", 0)], 3: [("add", 1)], 4: [("add", 2), ("stats2", 0)], 5: [("add", 3), ("stats2", 1)],
            6: [("newton2", 0)], 8: [("stats1", 0)], 9: [("stats1", 1)], 11: [("newton1", 0)],
            25: [("out", 0)], 26: [("out", 1)], 27: [("dt", 0)], 29: [("dt", 1)], 31: [("out", 2), ("out", 3)]}
POOL_PLAN = {28: [("u", 0)], 29: [("u", 1)], 30: [("u", 2)], 31: [("u", 3), ("reset", 0)]}
LN_VAR = 6
LN_STEPS = {1: LN_VAR + 5, 2: LN_VAR + 8}
PREPARED = (X_OUT - X_TURN1) // 2
FINISH = {"add", "turn2", "ffn", "out", "root2", "stats2", "newton2", "norm2"}


def x_start(u):
    return X_USES // 2 * (u - 1) + 2 * PREPARED


def scan_pass(nc, t, dram, mixed, before, rows_bc, out):
    with ExitStack() as ctx:
        sb = lambda n, s, d=F32: ctx.enter_context(nc.sbuf_tensor(n, s, d))
        sem = lambda n: ctx.enter_context(nc.semaphore(n))
        h_in = sb("s_h_in", [P, 2, 2, DIM])
        h1 = sb("s_h1", [P, 2, 2, DIM])
        xn = sb("s_xn", [P, 2, DIM])
        x_t = sb("s_x_t", [P, 2, ND, LEN])
        x2_t = sb("s_x2_t", [P, ND, LEN])
        y_t = sb("s_y_t", [P, ND, LEN])
        dt_t = sb("s_dt_t", [P, 2, ND, LEN])
        u_t = sb("s_u_t", [P, 2, ND, LEN])
        bc = sb("s_bc", [P, 2, 2 * NS, LEN])
        xp = sb("s_xp", [RANK + 2 * NS, LEN])
        dbx = sb("s_dbx", [P, 2, CW])
        hc = sb("s_hc", [P, 2, CW])
        stats = sb("s_stats", [P, 2, 2, 6])
        large = sb("s_large", [P, ND, 1])
        nudge = sb("s_nudge", [P, 1])
        small = {which: [sb(f"s_small{which}_{i}", [P, 2]) for i in range(8)] for which in (1, 2)}
        decay = ctx.enter_context(nc.psum_tensor("s_decay", [P, 2, 1024], F32))
        y_ps = ctx.enter_context(nc.psum_tensor("s_y_ps", [P, 512], F32))
        f_ps = ctx.enter_context(nc.psum_tensor("s_f_ps", [P, 512], F32))
        xch = [ctx.enter_context(nc.psum_tensor(f"s_xch{i}", [P, 512], F32)) for i in range(2)]

        decay_done, dbx_done, scan_done, hc_done, sum_done = (
            sem("s_decay_done"), sem("s_dbx_done"), sem("s_scan_done"), sem("s_hc_done"), sem("s_sum_done"))
        y_done = sem("s_y_done")
        x_full = [sem(f"s_x_full{i}") for i in range(2)]
        x_empty = [sem(f"s_x_empty{i}") for i in range(2)]
        f_full, f_empty = sem("s_f_full"), sem("s_f_empty")
        ln_step = {1: sem("s_ln1_step"), 2: sem("s_ln2_step")}
        root = {1: sem("s_root1"), 2: sem("s_root2")}
        norm_done = {1: sem("s_norm1"), 2: sem("s_norm2")}
        spread_out, large_set = sem("s_spread_out"), sem("s_large_set")
        bc_in = [sem(f"s_bc_in{i}") for i in range(2)]
        soft_step, dt_done, u_done, reset_done = sem("s_soft_step"), sem("s_dt_done"), sem("s_u_done"), sem("s_reset_done")
        loaded = [sem(f"s_loaded{i}") for i in range(2)]
        kept = [sem(f"s_kept{i}") for i in range(2)]
        stored = [sem(f"s_stored{i}") for i in range(2)]
        block = ctx.enter_context(nc.Block())

        def rows(k):
            return HEADS if k == 0 else TXT

        def cols(k):
            return slice(0, HEADS) if k == 0 else slice(HEADS, LEN)

        def run(engine, chunk, stages, plan, stages_first=False):
            def entry(u, par, xb, finish, prepare, out_use=X_OUT):
                for s in range(CHUNKS):
                    if not stages_first:
                        chunk(u, par, s)
                    for name, arg in plan.get(s, []):
                        if name in FINISH and finish:
                            stages[name](u - 1, 1 - par, arg, xb, out_use)
                        if name not in FINISH and prepare:
                            stages[name](u + 1, 1 - par, arg, xb, out_use)
                    if stages_first:
                        chunk(u, par, s)

            def alone(v, par, xb, names, out_use=X_OUT):
                for s in range(CHUNKS):
                    for name, arg in plan.get(s, []):
                        if (name in FINISH) == names:
                            stages[name](v, par, arg, xb, out_use)

            alone(0, 0, -(X_TURN1 // 2), False)
            entry(0, 0, PREPARED - X_TURN1 // 2, False, True)
            for u in (1, 2):
                entry(u, u % 2, x_start(u), True, True)
            with engine.Fori(0, (BATCH - 4) // 2) as i:
                entry(i * 2 + 3, 1, i * X_USES + x_start(3), True, True)
                entry(i * 2 + 4, 0, i * X_USES + x_start(4), True, True)
            u = BATCH - 1
            entry(u, u % 2, x_start(u), True, False, out_use=X_TURN1)
            return u, x_start(u) + (X_TURN1 + 4) // 2, alone

        def x_use(xb, k):
            return k % 2, xb + k // 2

        @block.sync
        def _(sp):
            def load(v, par, xb):
                if xb is not None:
                    for k in (2, 3):
                        b, c = x_use(xb, X_ADD + k)
                        wait(sp, x_empty[b], c + 1)
                sp.dma_start(h_in[:, par, 0, :], mixed[bass.ds(v, 1), :, :].rearrange("a p l -> (a p) l")).then_inc(loaded[par], 16)
                sp.dma_start(h_in[0:TXT, par, 1, :], dram["txt"][bass.ds(v, 1), :, :].rearrange("a p l -> (a p) l")).then_inc(loaded[par], 16)

            def save(v, par, target, signal):
                for k in range(2):
                    sp.dma_start(target[bass.ds(v, 1), cols(k), :].rearrange("a p l -> (a p) l"),
                                 h1[0:rows(k), par, k, :]).then_inc(signal, 16)

            def finish(v, par, xb, out_use):
                for k in (2, 3):
                    b, c = x_use(xb, X_ADD + k)
                    wait(sp, x_empty[b], c + 1)
                save(v, par, before, kept[par])

            def write(v, par, xb, out_use):
                for k in (2, 3):
                    b, c = x_use(xb, out_use + k)
                    wait(sp, x_empty[b], c + 1)
                save(v, par, out, stored[par])

            def spread(v, par, xb):
                b, c = x_use(xb, X_XPROJ)
                wait(sp, x_empty[b], c + 1)
                sp.dma_start(rows_bc[par:par + 1, :, :].rearrange("a n l -> (a n) l"), xp[RANK:, :]).then_inc(spread_out, 16)
                wait(sp, spread_out, v * 16 + 16)
                for k in range(2):
                    sp.dma_start(bc[:, par, NS * k:NS * k + NS, :],
                                 rows_bc[par:par + 1, NS * k:NS * k + NS, :].broadcast_to([P, NS, LEN])).then_inc(bc_in[par], 16)

            def entry(u, par, xb, prepare=True, out_use=X_OUT):
                finish(u - 1, 1 - par, xb, out_use)
                if prepare:
                    load(u + 1, 1 - par, xb)
                    spread(u + 1, 1 - par, xb)
                write(u - 1, 1 - par, xb, out_use)

            load(0, 0, None)
            load(1, 1, None)
            spread(0, 0, -(X_TURN1 // 2))
            spread(1, 1, PREPARED - X_TURN1 // 2)
            for u in (1, 2):
                entry(u, u % 2, x_start(u))
            with sp.Fori(0, (BATCH - 4) // 2) as i:
                entry(i * 2 + 3, 1, i * X_USES + x_start(3))
                entry(i * 2 + 4, 0, i * X_USES + x_start(4))
            u = BATCH - 1
            entry(u, u % 2, x_start(u), prepare=False, out_use=X_TURN1)
            xb = x_start(u) + (X_TURN1 + 4) // 2
            finish(u, u % 2, xb, X_TURN1)
            write(u, u % 2, xb, X_TURN1)
            for i in range(2):
                sp.wait_ge(kept[i], 32 * BATCH // 2)
                sp.wait_ge(stored[i], 32 * BATCH // 2)

        @block.tensor
        def _(pe):
            ident = t["ident"]

            def claim(xb, k):
                b, c = x_use(xb, k)
                wait(pe, x_empty[b], c)
                return xch[b], x_full[b]

            def chunk(u, par, s):
                wait(pe, hc_done, u * CHUNKS + s + 1)
                if s % 4 == 0:
                    wait(pe, y_done, u * ND + s // 4)
                for n in range(CN):
                    last = nc.tensor.matmul(y_ps[:, 0:LEN], ident[:, :], hc[:, s % 2, n * LEN:(n + 1) * LEN],
                                            start=(s % 4 == 0 and n == 0), stop=(s % 4 == 3 and n == CN - 1))
                last.then_inc(sum_done, 1)

            def add(v, par, r, xb, out_use):
                k, side = r // 2, r % 2
                bank, full = claim(xb, X_ADD + r)
                wait(pe, y_done, v * ND + (4 if side == 0 else ND))
                for j in range(4):
                    last = nc.tensor.transpose(bank[0:rows(k), P * j:P * j + P], x_t[:, par, 4 * side + j, cols(k)], ident[:, :])
                last.then_inc(full, 1)

            def turn(which, use, v, r, xb):
                bank, full = claim(xb, use + r)
                wait(pe, norm_done[which], v * 2 + 2)
                for j in range(2):
                    for k in range(2):
                        last = nc.tensor.transpose(bank[:, LEN * j + cols(k).start:LEN * j + cols(k).stop],
                                                   xn[0:rows(k), k, P * (2 * r + j):P * (2 * r + j) + P],
                                                   ident[0:rows(k), 0:rows(k)])
                last.then_inc(full, 1)

            def ffn(v, par, piece, xb, out_use):
                o, first, end = piece
                if first == 0:
                    wait(pe, f_empty, v * ND + o)
                if o == 0 and first == 0:
                    for k in (2, 3):
                        b, cc = x_use(xb, X_TURN2 + k)
                        wait(pe, x_empty[b], cc + 1)
                for i in range(first, end):
                    last = nc.tensor.matmul(f_ps[:, 0:LEN], t["w_low"][:, i, P * o:P * o + P], x2_t[:, i, :],
                                            start=(i == 0), stop=(i == ND - 1))
                if end == ND:
                    last.then_inc(f_full, 1)

            def finish(v, par, r, xb, out_use):
                side, k = r // 2, r % 2
                bank, full = claim(xb, out_use + r)
                wait(pe, f_empty, v * ND + 4 * side + 4)
                for j in range(4):
                    last = nc.tensor.transpose(bank[0:rows(k), P * j:P * j + P], y_t[:, 4 * side + j, cols(k)], ident[:, :])
                last.then_inc(full, 1)

            def xproj(v, par, piece, xb, out_use):
                first, end = piece
                if first == 0:
                    bank, full = claim(xb, X_XPROJ)
                    for k in (2, 3):
                        b, cc = x_use(xb, X_TURN1 + k)
                        wait(pe, x_empty[b], cc + 1)
                bank, full = xch[X_XPROJ % 2], x_full[X_XPROJ % 2]
                for i in range(first, end):
                    last = nc.tensor.matmul(bank[0:RANK + 2 * NS, 0:LEN], t["xpw_t"][:, i, :], x_t[:, par, i, :],
                                            start=(i == 0), stop=(i == ND - 1))
                if end == ND:
                    last.then_inc(full, 1)

            def dt_proj(v, par, r, xb, out_use):
                if r == 0:
                    b, c = x_use(xb, X_XPROJ)
                    wait(pe, x_empty[b], c + 1)
                bank, full = claim(xb, X_DT + r)
                for k, j in enumerate(DT_BLOCKS[r]):
                    last = nc.tensor.matmul(bank[:, LEN * k:LEN * k + LEN], t["dtw_t"][:, P * j:P * j + P],
                                            xp[0:RANK, :], start=True, stop=True)
                last.then_inc(full, 1)

            stages = {"add": add, "ffn": ffn, "out": finish, "xproj": xproj, "dt": dt_proj,
                      "turn2": lambda v, par, r, xb, *_: turn(2, X_TURN2, v, r, xb),
                      "turn1": lambda v, par, r, xb, *_: turn(1, X_TURN1, v, r, xb)}
            v, xb, alone = run(pe, chunk, stages, PE_PLAN, stages_first=True)
            alone(v, v % 2, xb, True, out_use=X_TURN1)

        @block.scalar
        def _(act):
            A = nc.scalar
            act.add_instruction(mybir.InstLoadActFuncSet(name=nc.get_next_instruction_name(), act_func_set_id=LN_EXP_TABLES))

            def take(xb, k):
                b, c = x_use(xb, k)
                wait(act, x_full[b], c + 1)
                return xch[b], x_empty[b]

            def chunk(u, par, s):
                j, n0 = s // 4, CN * (s % 4)
                wait(act, hc_done, u * CHUNKS + s - 1)
                if s == 0:
                    wait(act, reset_done, u + 1)
                for n in range(CN):
                    last = A.activation(decay[:, s % 2, n * LEN:(n + 1) * LEN], dt_t[:, par, j, :], ACT.Exp,
                                        scale=t["a_neg"][:, j, n0 + n:n0 + n + 1])
                last.then_inc(decay_done, 1)

            def roots(which, v):
                w = small[which]
                wait(act, ln_step[which], v * LN_STEPS[which] + LN_VAR)
                A.activation(w[1][:, :], w[0][:, :], ACT.Ln).then_inc(root[which], 1)
                wait(act, root[which], v * 2 + 1)
                A.activation(w[2][:, :], w[1][:, :], ACT.Exp, scale=-0.5).then_inc(root[which], 1)

            def turn2(v, par, r, xb, out_use):
                bank, empty = take(xb, X_TURN2 + r)
                A.activation(x2_t[:, 2 * r:2 * r + 2, :], bank[:, 0:2 * LEN].rearrange("p (j l) -> p j l", j=2),
                             ACT.Copy).then_inc(empty, 1)

            def turn1(v, par, r, xb, out_use):
                bank, empty = take(xb, X_TURN1 + r)
                A.activation(x_t[:, par, 2 * r:2 * r + 2, :], bank[:, 0:2 * LEN].rearrange("p (j l) -> p j l", j=2),
                             ACT.Copy).then_inc(empty, 1)

            def norm(which, v, par, k):
                src, rstd, shift = (h_in if which == 1 else h1), small[which][6], small[which][7]
                n = rows(k)
                if k == 0:
                    wait(act, ln_step[which], v * LN_STEPS[which] + LN_VAR + 5)
                A.activation(xn[0:n, k, :], src[0:n, par, k, :], ACT.Identity, scale=rstd[0:n, k:k + 1],
                             bias=shift[0:n, k:k + 1]).then_inc(norm_done[which], 1)

            def ffn(v, par, o, xb, out_use):
                wait(act, f_full, v * ND + o + 1)
                A.activation(y_t[:, o, :], f_ps[:, 0:LEN], ACT.Identity, bias=t["y_bias"][:, o:o + 1]).then_inc(f_empty, 1)

            def xproj(v, par, r, xb, out_use):
                bank, empty = take(xb, X_XPROJ)
                wait(act, spread_out, v * 16)
                A.activation(xp[:, :], bank[0:RANK + 2 * NS, 0:LEN], ACT.Copy).then_inc(empty, 1)

            def dt_bias(v, par, r, xb, out_use):
                bank, empty = take(xb, X_DT + r)
                for k, j in enumerate(DT_BLOCKS[r]):
                    last = A.activation(u_t[:, par, j, :], bank[:, LEN * k:LEN * k + LEN], ACT.Identity,
                                        bias=t["dt_bias"][:, j:j + 1])
                last.then_inc(empty, 1)

            def soft(v, par, piece, xb, out_use):
                half, step = piece
                d, z = dt_t[:, par, 4 * half:4 * half + 4, :], u_t[:, par, 4 * half:4 * half + 4, :]
                if step == 0:
                    for r in ((0, 1), (3, 4))[half]:
                        b, cc = x_use(xb, X_DT + r)
                        wait(act, x_empty[b], cc + 1)
                    A.activation(d, z, ACT.Abs).then_inc(soft_step, 1)
                else:
                    wait(act, soft_step, v * 6 + 3 * half + step)
                    if step == 1:
                        A.activation(d, d, ACT.Exp, scale=-1.0).then_inc(soft_step, 1)
                    else:
                        A.activation(d, d, ACT.Ln, bias=1.0).then_inc(soft_step, 1)

            stages = {"turn2": turn2, "turn1": turn1, "ffn": ffn, "xproj": xproj, "dt": dt_bias, "soft": soft,
                      "root2": lambda v, *_: roots(2, v), "root1": lambda v, *_: roots(1, v),
                      "norm2": lambda v, par, k, *_: norm(2, v, par, k), "norm1": lambda v, par, k, *_: norm(1, v, par, k)}
            v, xb, alone = run(act, chunk, stages, ACT_PLAN)
            alone(v, v % 2, xb, True, out_use=X_TURN1)

        @block.gpsimd
        def _(pool):
            def chunk(u, par, s):
                j, n0 = s // 4, CN * (s % 4)
                if s == 0:
                    wait(pool, u_done, u * 4 + 4)
                    wait(pool, bc_in[par], (u - par) * 16 + 32)
                wait(pool, scan_done, u * CHUNKS + s - 1)
                nc.gpsimd.tensor_tensor(dbx[:, s % 2, :].rearrange("p (n l) -> p n l", n=CN), bc[:, par, n0:n0 + CN, :],
                                        u_t[:, par, j, :].unsqueeze(1).broadcast_to([P, CN, LEN]), ALU.mult).then_inc(dbx_done, 1)

            def scaled_input(v, par, r, xb, out_use):
                if r % 2 == 0:
                    wait(pool, dt_done, v * 2 + r // 2 + 1)
                nc.gpsimd.tensor_tensor(u_t[:, par, 2 * r:2 * r + 2, :], dt_t[:, par, 2 * r:2 * r + 2, :],
                                        x_t[:, par, 2 * r:2 * r + 2, :], ALU.mult).then_inc(u_done, 1)

            def reset(v, par, r, xb, out_use):
                wait(pool, u_done, v * 4 + 4)
                nc.gpsimd.tensor_tensor(dt_t[:, par, :, 0:1], dt_t[:, par, :, 0:1], large[:, :, :], ALU.add).then_inc(reset_done, 1)

            nc.gpsimd.memset(large[:, :, :], RESET_DT).then_inc(large_set, 1)
            pool.wait_ge(large_set, 1)
            run(pool, chunk, {"u": scaled_input, "reset": reset}, POOL_PLAN)

        @block.vector
        def _(dve):
            V = nc.vector

            def take(xb, k):
                b, c = x_use(xb, k)
                wait(dve, x_full[b], c + 1)
                return xch[b], x_empty[b], c

            def block_output(u, par, j):
                wait(dve, sum_done, u * CHUNKS + 4 * j + 4)
                V.scalar_tensor_tensor(x_t[:, par, j, :], x_t[:, par, j, :], t["d_col"][:, j:j + 1], y_ps[:, 0:LEN],
                                       ALU.mult, ALU.add).then_inc(y_done, 1)

            def chunk(u, par, s):
                g = u * CHUNKS + s
                n0 = CN * (s % 4)
                wait(dve, decay_done, g + 1)
                wait(dve, dbx_done, g + 1)
                V.tensor_tensor_scan(out=decay[:, s % 2, 0:CW], data0=decay[:, s % 2, 0:CW], data1=dbx[:, s % 2, :],
                                     initial=0.0, op0=ALU.mult, op1=ALU.add).then_inc(scan_done, 1)
                wait(dve, sum_done, g - 1)
                wait(dve, scan_done, g + 1)
                V.tensor_tensor(hc[:, s % 2, :], decay[:, s % 2, 0:CW],
                                bc[:, par, NS + n0:NS + n0 + CN, :].rearrange("p n l -> p (n l)"), ALU.mult).then_inc(hc_done, 1)
                if s % 4 == 0 and s:
                    block_output(u, par, s // 4 - 1)
                elif s == 0 and not (isinstance(u, int) and u == 0):
                    block_output(u - 1, 1 - par, ND - 1)

            def add(v, par, r, xb, out_use):
                k, side = r // 2, r % 2
                bank, empty, c = take(xb, X_ADD + r)
                if r == 0:
                    wait(dve, stored[par], (v - par) * 16)
                V.tensor_tensor(h1[0:rows(k), par, k, 512 * side:512 * side + 512], bank[0:rows(k), :],
                                h_in[0:rows(k), par, k, 512 * side:512 * side + 512], ALU.add).then_inc(empty, 1)

            def ln_stats(which, v, par, tile, xb):
                src, mv, step = (h_in if which == 1 else h1), t[f"mv{which}"], ln_step[which]
                ve, base, n = small[which][0], v * LN_STEPS[which] + 3 * tile, rows(tile)
                if which == 1:
                    if tile == 0:
                        wait(dve, loaded[par], (v - par) * 16 + 32)
                else:
                    for k in (0, 1):
                        b, c = x_use(xb, X_ADD + 2 * tile + k)
                        wait(dve, x_empty[b], c + 1)
                for i in range(2):
                    last = V.bn_stats(stats[0:n, tile, i, :], src[0:n, par, tile, 512 * i:512 * i + 512])
                last.then_inc(step, 1)
                wait(dve, step, base + 1)
                V.memset(nudge[:, :], 0.0)
                V.bn_aggr(mv[0:n, tile, :], stats[0:n, tile, :, :].rearrange("p a b -> p (a b)")).then_inc(step, 1)
                wait(dve, step, base + 2)
                V.tensor_scalar(ve[:, tile:tile + 1], mv[:, tile, 1:2], EPS_LN, None, ALU.add).then_inc(step, 1)

            def newton(which, v):
                ve, _, r0, sq, pr, co, rstd, shift = (z[:, :] for z in small[which])
                step, base = ln_step[which], v * LN_STEPS[which] + LN_VAR
                wait(dve, root[which], v * 2 + 2)
                wait(dve, step, base)
                V.tensor_tensor(sq, r0, r0, ALU.mult).then_inc(step, 1)
                wait(dve, step, base + 1)
                V.tensor_tensor(pr, sq, ve, ALU.mult).then_inc(step, 1)
                wait(dve, step, base + 2)
                V.tensor_scalar(co, pr, -0.5, 1.5, ALU.mult, ALU.add).then_inc(step, 1)
                wait(dve, step, base + 3)
                V.tensor_tensor(rstd, co, r0, ALU.mult).then_inc(step, 1)
                wait(dve, step, base + 4)
                V.scalar_tensor_tensor(shift, t[f"mv{which}"][:, :, 0], -1.0, rstd, ALU.mult, ALU.mult).then_inc(step, 1)
                if which == 2:
                    row_norms(v)

            def row_norms(v):
                sq, pr, rstd = small[2][3], small[2][4], small[2][6]
                step, base = ln_step[2], v * LN_STEPS[2] + LN_VAR + 5
                V.tensor_tensor(sq[:, :], rstd[:, :], rstd[:, :], ALU.mult).then_inc(step, 1)
                wait(dve, step, base + 1)
                V.tensor_tensor(pr[:, :], sq[:, :], t["mv2"][:, :, 1], ALU.mult).then_inc(step, 1)
                wait(dve, step, base + 2)
                V.scalar_tensor_tensor(t["over"][:, :], pr[:, :], float(DIM), t["over"][:, :], ALU.mult, ALU.max).then_inc(step, 1)

            def dt_total(v, par, half, xb, out_use):
                wait(dve, soft_step, v * 6 + 3 * half + 3)
                d, z = (a[:, par, 4 * half:4 * half + 4, :].rearrange("p j l -> p (j l)") for a in (dt_t, u_t))
                V.scalar_tensor_tensor(d, z, 0.0, d, ALU.max, ALU.add).then_inc(dt_done, 1)

            def finish(v, par, r, xb, out_use):
                side, k = r // 2, r % 2
                bank, empty, c = take(xb, out_use + r)
                if r == 0:
                    wait(dve, kept[par], (v - par) * 16 + 32)
                V.tensor_tensor(h1[0:rows(k), par, k, 512 * side:512 * side + 512], bank[0:rows(k), :],
                                h1[0:rows(k), par, k, 512 * side:512 * side + 512], ALU.add).then_inc(empty, 1)

            stages = {"add": add, "dt": dt_total, "out": finish,
                      "stats1": lambda v, par, k, xb, *_: ln_stats(1, v, par, k, xb),
                      "stats2": lambda v, par, k, xb, *_: ln_stats(2, v, par, k, xb),
                      "newton1": lambda v, *_: newton(1, v), "newton2": lambda v, *_: newton(2, v)}
            v, xb, alone = run(dve, chunk, stages, DVE_PLAN)
            block_output(v, v % 2, ND - 1)
            alone(v, v % 2, xb, True, out_use=X_TURN1)


def general_path(nc, t, dram, before, out):
    any_over(nc, t)
    with ExitStack() as ctx:
        general_weights(nc, t, dram, t["flag"], ctx)
        general_rows(nc, t, t["flag"], before, out)


def any_over(nc, t):
    with ExitStack() as ctx:
        sb = lambda n, s, d=F32: ctx.enter_context(nc.sbuf_tensor(n, s, d))
        pb = lambda n, s: ctx.enter_context(nc.psum_tensor(n, s, F32))
        sem = lambda n: ctx.enter_context(nc.semaphore(n))
        seen = sb("g_seen", [P, 2])
        ones = sb("g_ones", [P, 1])
        count = sb("g_count", [1, 1])
        count_ps = pb("g_count_ps", [P, 512])
        step, counted = sem("g_step"), sem("g_counted")
        block = ctx.enter_context(nc.Block())

        @block.vector
        def _(dve):
            n = [0]
            V = nc.vector
            V.memset(ones[:, :], 1.0)
            V.tensor_scalar(seen[:, :], t["over"][:, :], NORM_LIMIT * NORM_LIMIT, None, ALU.is_gt).then_inc(step, 1)
            dve.wait_ge(counted, 1)
            n[0] = 1
            link(dve, step, n, V.reduce_sum(count[:, :], count_ps[0:1, 0:2], mybir.AxisListType.X))
            link(dve, step, n, V.tensor_copy(t["flag"][:, :], count[:, :]))

        @block.tensor
        def _(pe):
            pe.wait_ge(step, 1)
            nc.tensor.matmul(count_ps[0:1, 0:2], ones[:, :], seen[:, :], start=True, stop=True).then_inc(counted, 1)



def general_weights(nc, t, dram, flag, outer):
    t["w_high"] = outer.enter_context(nc.sbuf_tensor("w_high", [P, ND, DIM], F32))
    with ExitStack() as ctx:
        sb = lambda n, s, d=F32: ctx.enter_context(nc.sbuf_tensor(n, s, d))
        pb = lambda n, s: ctx.enter_context(nc.psum_tensor(n, s, F32))
        sem = lambda n: ctx.enter_context(nc.semaphore(n))
        qw = sb("h_qw", [P, 8, ND, 32], I32)
        part = sb("h_part", [P, 4, 256], I32)
        word = sb("h_word", [P, 4, 256], I32)
        wide = sb("h_wide", [P, 256, 32], I32)
        codes = [sb(f"h_codes{i}", [P, 256 * 32], BF16) for i in range(2)]
        tables = sb("h_tables", [P, P, 16])
        square = sb("h_square", [P, 8, 16])
        hot = [sb(f"h_hot{i}", [P, DIM]) for i in range(2)]
        picked = sb("h_picked", [P, DIM])
        rep = [pb(f"h_rep{i}", [P, DIM]) for i in range(2)]
        row_ps = pb("h_row_ps", [P, DIM])
        sum_ps = pb("h_sum_ps", [P, 512])
        loaded, dve_step, ready = sem("h_loaded"), sem("h_dve_step"), sem("h_ready")
        repeated, hot_done, rowed, picked_done, summed, stored = (
            sem("h_repeated"), sem("h_hot_done"), sem("h_rowed"), sem("h_picked_done"), sem("h_summed"), sem("h_stored"))
        block = ctx.enter_context(nc.Block())

        @block.sync
        def _(sp):
            go = sp.value_load(flag[0:1, 0:1])
            with sp.If(go != 0):
                sp.dma_start(qw[:, :, :, :], dram["qweight"].rearrange("b (t p) w -> p b t w", p=P)).then_inc(loaded, 16)
                for o in range(8):
                    sp.dma_start(tables[16 * o:16 * o + 16, :, :],
                                 dram["lut8"].rearrange("(g o) (a b) -> o a g b", o=8, a=16)[o]).then_inc(loaded, 16)
                sp.wait_ge(loaded, 144)

        @block.vector
        def _(dve):
            V = nc.vector
            go = dve.value_load(flag[0:1, 0:1])
            with dve.If(go != 0):
                n = [0]
                dve.wait_ge(loaded, 144)
                for i in range(2):
                    weight_codes(nc, dve, dve_step, n, qw, part, word, wide, codes[i], range(4 * i, 4 * i + 4))
                V.memset(part[:, 0, 0:1], 0).then_inc(ready, 1)
                V.memset(part[:, 1, 0:1], 0).then_inc(stored, 1)
                with dve.Fori(0, ND) as o:
                    for j in range(16):
                        g = o * 16 + j
                        dve.wait_ge(repeated, g + 1)
                        for i in range(2):
                            V.tensor_scalar(hot[i][:, :], rep[i][:, :], t["code_col"][:, 0:1], None, ALU.is_equal)
                        V.tensor_tensor(square[:, :, :], tables[:, bass.ds(g, 1), :].broadcast_to([P, 8, 16]),
                                        t["sel8"][:, :].unsqueeze(2).broadcast_to([P, 8, 16]), ALU.mult).then_inc(hot_done, 1)
                        dve.wait_ge(hot_done, g + 1)
                        dve.wait_ge(rowed, g + 1)
                        V.tensor_tensor(picked[:, :], row_ps[:, :], hot[0][:, :], ALU.mult).then_inc(picked_done, 1)
                        dve.wait_ge(summed, g + 1)
                        V.tensor_scalar(t["w_high"][:, :, bass.ds(o * P + 8 * j, 8)],
                                        sum_ps[:, 0:64].rearrange("p (i c) -> p i c", i=ND), 1.0, None, ALU.mult).then_inc(stored, 1)

        @block.tensor
        def _(pe):
            go = pe.value_load(flag[0:1, 0:1])
            with pe.If(go != 0):
                pe.wait_ge(ready, 1)
                with pe.Fori(0, ND) as o:
                    for j in range(16):
                        g = o * 16 + j
                        pe.wait_ge(stored, g + 1)
                        for i in range(2):
                            for half in range(2):
                                last = nc.tensor.matmul(rep[i][:, 512 * half:512 * half + 512], t["spread"][:, P * j:P * j + P],
                                                        codes[i][:, bass.ds(o * DIM + 512 * half, 512)], start=True, stop=True)
                        last.then_inc(repeated, 1)
                        pe.wait_ge(hot_done, g + 1)
                        for half in range(2):
                            last = nc.tensor.matmul(row_ps[:, 512 * half:512 * half + 512], square[:, :, :].rearrange("p a b -> p (a b)"),
                                                    hot[1][:, 512 * half:512 * half + 512], start=True, stop=True)
                        last.then_inc(rowed, 1)
                        pe.wait_ge(picked_done, g + 1)
                        for i in range(ND):
                            last = nc.tensor.matmul(sum_ps[:, 8 * i:8 * i + 8], picked[:, P * i:P * i + P], t["sel8"][:, :],
                                                    start=True, stop=True)
                        last.then_inc(summed, 1)


def general_rows(nc, t, flag, before, out):
    with ExitStack() as ctx:
        sb = lambda n, s, d=F32: ctx.enter_context(nc.sbuf_tensor(n, s, d))
        pb = lambda n, s: ctx.enter_context(nc.psum_tensor(n, s, F32))
        sem = lambda n: ctx.enter_context(nc.semaphore(n))
        h1 = sb("r_h1", [P, 2, DIM])
        low = sb("r_low", [P, 2, DIM])
        xn = sb("r_xn", [P, 2, DIM])
        x2_t = sb("r_x2_t", [P, ND, LEN])
        y_t = sb("r_y_t", [P, ND, LEN])
        stats = sb("r_stats", [P, 2, 2, 6])
        mv = sb("r_mv", [P, 2, 2])
        ve, ln, r0, sq, pr, co, rstd, mask, other = (sb(f"r_small{i}", [P, 2]) for i in range(9))
        xp = pb("r_xp", [P, 512])
        fp = pb("r_fp", [P, 512])
        op = pb("r_op", [P, 512])
        loaded, written = sem("r_loaded"), sem("r_written")
        dve_step, root, turned, taken, multiplied, y_done, back, added = (
            sem("r_dve_step"), sem("r_root"), sem("r_turned"), sem("r_taken"), sem("r_multiplied"), sem("r_y_done"),
            sem("r_back"), sem("r_added"))
        rows = (HEADS, TXT)
        cols = (slice(0, HEADS), slice(HEADS, LEN))
        DVE_STEPS = 15
        block = ctx.enter_context(nc.Block())

        def entry(ap, v, k):
            return ap[bass.ds(v, 1), cols[k], :].rearrange("a p l -> (a p) l")

        @block.sync
        def _(sp):
            go = sp.value_load(flag[0:1, 0:1])
            with sp.If(go != 0):
                def one(v):
                    wait(sp, written, v * 32)
                    for k in range(2):
                        sp.dma_start(h1[0:rows[k], k, :], entry(before, v, k)).then_inc(loaded, 16)
                        sp.dma_start(low[0:rows[k], k, :], entry(out, v, k)).then_inc(loaded, 16)
                    sp.wait_ge(dve_step, (v + 1) * DVE_STEPS)
                    for k in range(2):
                        sp.dma_start(entry(out, v, k), low[0:rows[k], k, :]).then_inc(written, 16)

                one(0)
                with sp.Fori(1, BATCH) as v:
                    one(v)
                sp.wait_ge(written, 32 * BATCH)

        @block.vector
        def _(dve):
            V = nc.vector
            go = dve.value_load(flag[0:1, 0:1])
            with dve.If(go != 0):
                V.memset(mv[:, :, :], 1.0).then_inc(added, 1)
                with dve.Fori(0, BATCH) as v:
                    done = [0]

                    def step(ins):
                        done[0] += 1
                        ins.then_inc(dve_step, 1)
                        dve.wait_ge(dve_step, v * DVE_STEPS + done[0])

                    dve.wait_ge(loaded, v * 64 + 64)
                    for k in range(2):
                        for i in range(2):
                            last = V.bn_stats(stats[0:rows[k], k, i, :], h1[0:rows[k], k, 512 * i:512 * i + 512])
                    step(last)
                    step(V.memset(ve[:, :], 1.0))
                    V.memset(ln[:, :], 1.0)
                    for k in range(2):
                        last = V.bn_aggr(mv[0:rows[k], k, :], stats[0:rows[k], k, :, :].rearrange("p a b -> p (a b)"))
                    step(last)
                    step(V.tensor_scalar(ve[:, :], mv[:, :, 1], EPS_LN, None, ALU.add))
                    dve.wait_ge(root, v * 2 + 2)
                    step(V.tensor_tensor(sq[:, :], r0[:, :], r0[:, :], ALU.mult))
                    step(V.tensor_tensor(pr[:, :], sq[:, :], ve[:, :], ALU.mult))
                    step(V.tensor_scalar(co[:, :], pr[:, :], -0.5, 1.5, ALU.mult, ALU.add))
                    step(V.tensor_tensor(rstd[:, :], co[:, :], r0[:, :], ALU.mult))
                    step(V.tensor_tensor(sq[:, :], rstd[:, :], rstd[:, :], ALU.mult))
                    step(V.tensor_tensor(pr[:, :], sq[:, :], mv[:, :, 1], ALU.mult))
                    step(V.tensor_scalar(mask[:, :], pr[:, :], float(DIM), NORM_LIMIT * NORM_LIMIT, ALU.mult, ALU.is_gt))
                    step(V.tensor_scalar(other[:, :], mask[:, :], -1.0, 1.0, ALU.mult, ALU.add))
                    for k in range(2):
                        last = V.tensor_scalar(xn[0:rows[k], k, :], h1[0:rows[k], k, :], mv[0:rows[k], k, 0:1],
                                               rstd[0:rows[k], k:k + 1], ALU.subtract, ALU.mult)
                    step(last)
                    for k in range(2):
                        last = V.tensor_scalar(low[0:rows[k], k, :], low[0:rows[k], k, :], other[0:rows[k], k:k + 1], None, ALU.mult)
                    step(last)
                    for r in range(4):
                        dve.wait_ge(turned, v * 4 + r + 1)
                        V.tensor_scalar(x2_t[:, 2 * r:2 * r + 2, :], xp[:, 0:2 * LEN].rearrange("p (j l) -> p j l", j=2),
                                        1.0, None, ALU.mult).then_inc(taken, 1)
                    for r in range(4):
                        side, k = r // 2, r % 2
                        part = slice(512 * side, 512 * side + 512)
                        dve.wait_ge(back, v * 4 + r + 1)
                        V.tensor_tensor(h1[0:rows[k], k, part], h1[0:rows[k], k, part], op[0:rows[k], :], ALU.add).then_inc(added, 1)
                        if r == 3:
                            dve.wait_ge(added, v * 4 + 5)
                    for k in range(2):
                        last = V.scalar_tensor_tensor(low[0:rows[k], k, :], h1[0:rows[k], k, :], mask[0:rows[k], k:k + 1],
                                                      low[0:rows[k], k, :], ALU.mult, ALU.add)
                    step(last)
                    assert done[0] == DVE_STEPS, done

        @block.scalar
        def _(act):
            A = nc.scalar
            go = act.value_load(flag[0:1, 0:1])
            with act.If(go != 0):
                with act.Fori(0, BATCH) as v:
                    act.wait_ge(dve_step, v * DVE_STEPS + 4)
                    A.activation(ln[:, :], ve[:, :], ACT.Ln).then_inc(root, 1)
                    act.wait_ge(root, v * 2 + 1)
                    A.activation(r0[:, :], ln[:, :], ACT.Exp, scale=-0.5).then_inc(root, 1)
                    for o in range(ND):
                        act.wait_ge(multiplied, v * ND + o + 1)
                        A.activation(y_t[:, o, :], fp[:, 0:LEN], ACT.Identity, bias=t["y_bias"][:, o:o + 1]).then_inc(y_done, 1)

        @block.tensor
        def _(pe):
            ident = t["ident"]
            go = pe.value_load(flag[0:1, 0:1])
            with pe.If(go != 0):
                with pe.Fori(0, BATCH) as v:
                    pe.wait_ge(dve_step, v * DVE_STEPS + DVE_STEPS - 1)
                    for r in range(4):
                        if r:
                            pe.wait_ge(taken, v * 4 + r)
                        for j in range(2):
                            for k in range(2):
                                last = nc.tensor.transpose(xp[:, LEN * j + cols[k].start:LEN * j + cols[k].stop],
                                                           xn[0:rows[k], k, P * (2 * r + j):P * (2 * r + j) + P],
                                                           ident[0:rows[k], 0:rows[k]])
                        last.then_inc(turned, 1)
                    pe.wait_ge(taken, v * 4 + 4)
                    for o in range(ND):
                        if o:
                            pe.wait_ge(y_done, v * ND + o)
                        for i in range(ND):
                            last = nc.tensor.matmul(fp[:, 0:LEN], t["w_high"][:, i, P * o:P * o + P], x2_t[:, i, :],
                                                    start=(i == 0), stop=(i == ND - 1))
                        last.then_inc(multiplied, 1)
                    pe.wait_ge(y_done, v * ND + ND)
                    for r in range(4):
                        side, k = r // 2, r % 2
                        if r:
                            pe.wait_ge(added, v * 4 + r + 1)
                        for j in range(4):
                            last = nc.tensor.transpose(op[0:rows[k], P * j:P * j + P], y_t[:, 4 * side + j, cols[k]], ident[:, :])
                        last.then_inc(back, 1)


def persistent(nc, ctx):
    t = {}
    for name, shape, dtype in (
            ("ident", [P, P], F32), ("sel8", [P, 8], F32), ("code_col", [P, 1], F32), ("ramp", [P, HALF], F32),
            ("spread", [P, 16 * P], BF16), ("lut_t", [P, P], F32),
            ("a_neg", [P, ND, NS], F32), ("d_col", [P, ND], F32), ("dt_bias", [P, ND], F32), ("y_bias", [P, ND], F32),
            ("xpw_t", [P, ND, 2 * RANK], F32), ("dtw_t", [RANK, DIM], F32), ("mv1", [P, 2, 2], F32), ("mv2", [P, 2, 2], F32),
            ("over", [P, 2], F32), ("flag", [1, 1], I32)):
        t[name] = ctx.enter_context(nc.sbuf_tensor(name, shape, dtype))
    return t


def build(nc, dram, out):
    mixed = nc.dram_tensor("mixed", (BATCH, HEADS, LK), F32, kind="Internal").ap()
    before = nc.dram_tensor("before", (BATCH, LEN, DIM), F32, kind="Internal").ap()
    rows_bc = nc.dram_tensor("rows_bc", (2, 2 * NS, LEN), F32, kind="Internal").ap()
    with ExitStack() as ctx:
        t = persistent(nc, ctx)
        constants(nc, t, dram)
        token_mixer(nc, t, dram, mixed)
        with ExitStack() as low:
            t["w_low"] = low.enter_context(nc.sbuf_tensor("w_low", [P, ND, DIM], F32))
            dense_weights(nc, t, dram)
            scan_pass(nc, t, dram, mixed, before, rows_bc, out)
        general_path(nc, t, dram, before, out)


_NAMES = {"x": "x", "txt": "txt", "L0_tok_log_dt": "log_dt", "L0_tok_Lambda": "Lambda",
          "L0_attn_A_log": "A_log", "L0_attn_D": "D", "L0_attn_x_proj_w": "x_proj_w",
          "L0_attn_dt_proj_w": "dt_proj_w", "L0_attn_dt_proj_b": "dt_proj_b",
          "L0_ffn_qweight": "qweight", "L0_ffn_lut4": "lut4", "L0_ffn_lut8": "lut8", "L0_ffn_bias": "bias"}


def kernel(**inputs):
    import numpy as _np
    import concourse.bacc as _bacc
    from concourse import mybir as _mybir
    from concourse.bass_utils import run_bass_kernel_spmd as _run

    nc = _bacc.Bacc("TRN2", target_bir_lowering=False, num_devices=1)
    arrays, dram = {}, {}
    for name, short in _NAMES.items():
        a = _np.ascontiguousarray(inputs[name])
        arrays[f"in_{name}"] = a
        dram[short] = nc.dram_tensor(f"in_{name}", a.shape, _mybir.dt.from_np(a.dtype), kind="ExternalInput").ap()
    out = nc.dram_tensor("out_0", (BATCH, LEN, DIM), _mybir.dt.float32, kind="ExternalOutput").ap()
    build(nc, dram, out)
    r = _run(nc, [arrays], core_ids=[0])
    return r.results[0]["out_0"]
```

```python
import math
from contextlib import ExitStack

import concourse.bass as bass
from concourse import mybir

F32 = mybir.dt.float32
BF16 = mybir.dt.bfloat16
I32 = mybir.dt.int32
ALU = mybir.AluOpType
ACT = mybir.ActivationFunctionType

P = 128
BATCH, HEADS, MODES, LK = 64, 128, 64, 1024
TXT = 77
LEN = HEADS + TXT
DIM = 1024
ND = DIM // P
NS = 16
RANK = 32
HALF = LK // 2
EPS_TOK, EPS_LN = 1e-7, 1e-5
ROUND = 1.5 * 2.0 ** 23
INV_TURN = 1.0 / (2.0 * math.pi)
TURN = 6.283185
RESET_DT = 1e37
A_MOST = -1e-30
NORM_LIMIT = 64.0

HG = 8
NG = HEADS // HG
CN = 4
CW = CN * LEN
CHUNKS = ND * NS // CN
LN_EXP_TABLES = 6


def wait(engine, sem, value):
    if isinstance(value, int) and value <= 0:
        return
    engine.wait_ge(sem, value)


def link(engine, sem, counter, instruction):
    counter[0] += 1
    instruction.then_inc(sem, 1)
    engine.wait_ge(sem, counter[0])


def constants(nc, t, dram, kept):
    with ExitStack() as ctx:
        sb = lambda n, s, d=F32: ctx.enter_context(nc.sbuf_tensor(n, s, d))
        sem = lambda n: ctx.enter_context(nc.semaphore(n))
        zero = sb("c_zero", [P, P])
        wide = sb("c_wide", [P, 8])
        row = sb("c_row", [P, 1], I32)
        row15 = sb("c_row15", [P, 1], I32)
        col = sb("c_col", [P, HALF], I32)
        xpw = sb("c_xpw", [2 * RANK, DIM])
        dtw = sb("c_dtw", [P, ND, RANK])
        spread = sb("c_spread", [P, 16 * P], BF16)
        vec = sb("c_vec", [3 * ND, P])
        ps = [ctx.enter_context(nc.psum_tensor(f"c_ps{i}", [P, 512], F32)) for i in range(4)]
        loaded, alog_in = sem("c_loaded"), sem("c_alog_in")
        pool_step, dve_step, built = sem("c_pool_step"), sem("c_dve_step"), sem("c_built")
        exp_done, tables_made = sem("c_exp_done"), sem("c_tables_made")
        turned, copied = sem("c_turned"), sem("c_copied")
        block = ctx.enter_context(nc.Block())

        @block.sync
        def _(sp):
            sp.dma_start(t["a_neg"][:, :, :], dram["A_log"].rearrange("(j p) n -> p j n", p=P)).then_inc(alog_in, 16)
            sp.dma_start(xpw[:, :], dram["x_proj_w"]).then_inc(loaded, 16)
            sp.dma_start(dtw[:, :, :], dram["dt_proj_w"].rearrange("(j p) r -> p j r", p=P)).then_inc(loaded, 16)
            for k, src in enumerate(("D", "dt_proj_b", "bias")):
                sp.dma_start(vec[ND * k:ND * k + ND, :], dram[src].rearrange("(j p) -> j p", p=P)).then_inc(loaded, 16)
            sp.wait_ge(tables_made, 1)
            sp.dma_start(kept["spread"], spread[:, :]).then_inc(loaded, 16)
            sp.wait_ge(loaded, 16 * 6)

        @block.gpsimd
        def _(pool):
            n = [0]
            link(pool, pool_step, n, nc.gpsimd.memset(zero[:, :], 0.0))
            link(pool, pool_step, n, nc.gpsimd.affine_select(
                out=t["ident"][:, :], in_=zero[:, :], compare_op=ALU.not_equal, fill=1.0, base=0,
                pattern=[[-1, P]], channel_multiplier=1))
            link(pool, pool_step, n, nc.gpsimd.memset(wide[:, :], 1.0))
            link(pool, pool_step, n, nc.gpsimd.affine_select(
                out=wide[:, :], in_=wide[:, :], compare_op=ALU.is_ge, fill=0.0, base=0,
                pattern=[[-16, 8]], channel_multiplier=1))
            link(pool, pool_step, n, nc.gpsimd.affine_select(
                out=t["sel8"][:, :], in_=wide[:, :], compare_op=ALU.is_ge, fill=0.0, base=15,
                pattern=[[16, 8]], channel_multiplier=-1))
            nc.gpsimd.iota(row[:, :], pattern=[[0, 1]], base=0, channel_multiplier=1).then_inc(built, 1)
            nc.gpsimd.iota(col[:, :], pattern=[[1, HALF]], base=0, channel_multiplier=0).then_inc(built, 1)

        @block.scalar
        def _(act):
            act.wait_ge(alog_in, 16)
            nc.scalar.activation(t["a_neg"][:, :, :], t["a_neg"][:, :, :], ACT.Exp).then_inc(exp_done, 1)

        @block.tensor
        def _(pe):
            pe.wait_ge(built, 2)
            pe.wait_ge(loaded, 16 * 5)
            ident = t["ident"]
            for j in range(ND):
                last = nc.tensor.transpose(ps[0][:, 64 * j:64 * j + 64], xpw[:, P * j:P * j + P], ident[0:64, 0:64])
            last.then_inc(turned, 1)
            for j in range(ND):
                last = nc.tensor.transpose(ps[1 + j // 4][0:RANK, P * (j % 4):P * (j % 4) + P], dtw[:, j, :], ident[:, :])
            last.then_inc(turned, 1)
            nc.tensor.transpose(ps[3][:, 0:3 * ND], vec[:, :], ident[0:3 * ND, 0:3 * ND]).then_inc(turned, 1)

        @block.vector
        def _(dve):
            n = [0]
            dve.wait_ge(built, 2)
            ident = t["ident"]
            link(dve, dve_step, n, nc.vector.tensor_scalar(row15[:, :], row[:, :], 15, None, ALU.bitwise_and))
            link(dve, dve_step, n, nc.vector.tensor_copy(t["code_col"][:, :], row15[:, :]))
            link(dve, dve_step, n, nc.vector.tensor_copy(t["ramp"][:, :], col[:, :]))
            for c0 in range(0, P, 32):
                link(dve, dve_step, n, nc.vector.tensor_copy(
                    spread[:, 16 * c0:16 * (c0 + 32)].rearrange("p (c b) -> p c b", b=16),
                    ident[:, c0:c0 + 32].unsqueeze(2).broadcast_to([P, 32, 16])))
            for buf in ("mv1", "mv2"):
                link(dve, dve_step, n, nc.vector.memset(t[buf][:, :, :], 1.0))
            link(dve, dve_step, n, nc.vector.memset(t["over"][:, :], 0.0))
            dve.wait_ge(exp_done, 1)
            link(dve, dve_step, n, nc.vector.tensor_scalar(
                t["a_neg"][:, :, :], t["a_neg"][:, :, :], -1.0, A_MOST, ALU.mult, ALU.min))
            dve.wait_ge(turned, 3)
            xt = ps[0][:, :].rearrange("p (j r) -> p j r", j=ND)
            link(dve, dve_step, n, nc.vector.tensor_copy(t["xpw_t"][:, :, :], xt))
            for k in range(2):
                link(dve, dve_step, n, nc.vector.tensor_copy(t["dtw_t"][:, 512 * k:512 * k + 512], ps[1 + k][0:RANK, :]))
            for k, name in enumerate(("d_col", "dt_bias", "y_bias")):
                link(dve, dve_step, n, nc.vector.tensor_copy(t[name][:, :], ps[3][:, ND * k:ND * k + ND]))
            nc.vector.memset(zero[:, 0:1], 0.0).then_inc(tables_made, 1)


def token_mixer(nc, t, dram, mixed):
    x = dram["x"].rearrange("c h n r -> c h (n r)")
    with ExitStack() as ctx:
        sb = lambda n, s, d=F32: ctx.enter_context(nc.sbuf_tensor(n, s, d))
        sem = lambda n: ctx.enter_context(nc.semaphore(n))
        pb = lambda n: ctx.enter_context(nc.psum_tensor(n, [P, 512], F32))
        ldt = sb("t_ldt", [P, 2 * HEADS])
        dt = sb("t_dt", [P, 2 * HEADS])
        lam = sb("t_lam", [P, 2])
        growing = sb("t_growing", [P, 1])
        sgn = sb("t_sgn", [P, 1])
        at = sb("t_at", [P, 4])
        role = sb("t_role", [P, 2])
        pos = sb("t_pos", [P, HALF])
        rate = sb("t_rate", [P, HEADS])
        freq = sb("t_freq", [P, HEADS])
        turns = sb("t_turns", [P, HEADS])
        ea = sb("t_ea", [P, 4, HEADS])
        aa = sb("t_aa", [P, 4, HEADS])
        yy = sb("t_yy", [P, 2, 4, HEADS])
        kk = sb("t_kk", [P, 2, 4, HEADS])
        re = sb("t_re", [P, 4, HEADS])
        im = sb("t_im", [P, 4, HEADS])
        w = [sb(f"t_w{i}", [P, HEADS]) for i in range(10)]
        gre = sb("t_gre", [P, 2, HEADS])
        gim = sb("t_gim", [P, 2, HEADS])
        xg = sb("t_xg", [BATCH, 2, HG * 128])
        xs = sb("t_xs", [BATCH, 2, 2, HG, 2, MODES])
        mm1 = sb("t_mm1", [P, 2, HG, BATCH])
        mm2 = sb("t_mm2", [P, 2, HG, BATCH])
        gw = sb("t_gw", [P, 2, HG, 2, BATCH])
        ang = sb("t_ang", [P, HG * HALF])
        near = sb("t_near", [P, HG * HALF])
        mag = sb("t_mag", [P, 2, HG * HALF])
        osc = sb("t_osc", [P, HG * HALF])
        res = sb("t_res", [P, 2, HG, HALF])
        wa, wb = pb("t_wa"), pb("t_wb")
        kb = [pb(f"t_kb{i}") for i in range(4)]
        loaded, dve_step = sem("t_loaded"), sem("t_dve_step")
        dt_exp, arg_ready, arg_done = sem("t_dt_exp"), sem("t_arg_ready"), sem("t_arg_done")
        params = sem("t_params")
        x_in = [sem(f"t_x_in{i}") for i in range(2)]
        swapped, w_turned, w_read, scaled = sem("t_swapped"), sem("t_w_turned"), sem("t_w_read"), sem("t_scaled")
        turned, rounded, reduced = sem("t_turned"), sem("t_rounded"), sem("t_reduced")
        g_half = sem("t_g_half")
        mag_done, sine_done, table = sem("t_mag_done"), sem("t_sine_done"), sem("t_table")
        full = [sem(f"t_full{i}") for i in range(4)]
        empty = [sem(f"t_empty{i}") for i in range(4)]
        out_done = [sem(f"t_out_done{i}") for i in range(2)]
        block = ctx.enter_context(nc.Block())

        def loop(engine, step, tail=None):
            for G in range(4):
                step(G, G % 2, G == 0)
            with engine.Fori(2, NG // 2) as i:
                step(i * 2, 0, False)
                step(i * 2 + 1, 1, False)
            if tail:
                tail(NG - 1, (NG - 1) % 2)

        def out_count(G, half):
            return 16 * (G - half)

        @block.sync
        def _(sp):
            sp.dma_start(ldt[:, :], dram["log_dt"].rearrange("h r -> (h r)").unsqueeze(0).broadcast_to([P, 2 * HEADS])).then_inc(loaded, 16)
            for k in range(2):
                sp.dma_start(lam[64 * k:64 * k + 64, :], dram["Lambda"]).then_inc(loaded, 16)

            def load(G, half, i):
                wait(sp, swapped, G - 1)
                sp.dma_start(xg[:, half, :].rearrange("c (h m) -> c h m", h=HG), x[:, bass.ds(G * HG, HG), :]).then_inc(x_in[half], 16)

            def store(G, half, i):
                for b in range(4):
                    wait(sp, empty[b], 2 * G + 2)
                for a in range(2):
                    sp.dma_start(mixed[:, bass.ds(G * HG, HG), a * HALF:(a + 1) * HALF],
                                 res[64 * a:64 * a + 64, half, :, :]).then_inc(out_done[half], 16)

            load(0, 0, 0)
            load(1, 1, 0)
            with sp.Fori(1, NG // 2) as i:
                load(i * 2, 0, i)
                store(i * 2 - 2, 0, i)
                load(i * 2 + 1, 1, i)
                store(i * 2 - 1, 1, i)
            store(NG - 2, 0, 0)
            store(NG - 1, 1, 0)
            for half in range(2):
                sp.wait_ge(out_done[half], 32 * (NG // 2))

        @block.scalar
        def _(act):
            act.wait_ge(loaded, 48)
            nc.scalar.activation(dt[:, :], ldt[:, :], ACT.Exp).then_inc(dt_exp, 1)
            act.wait_ge(arg_ready, 1)
            nc.scalar.activation(ea[:, :, :], ea[:, :, :], ACT.Exp).then_inc(arg_done, 1)
            nc.scalar.activation(yy[:, :, :, :], yy[:, :, :, :], ACT.Sin, scale=TURN).then_inc(arg_done, 1)
            act.wait_ge(params, 1)

            def evacuate(G, half):
                wait(act, out_done[half], out_count(G, half))
                for h in range(0, HG, 2):
                    b = h % 4
                    act.wait_ge(full[b], 2 * G + h // 4 + 1)
                    nc.scalar.activation(res[:, half, h, :], kb[b][:, :], ACT.Copy).then_inc(empty[b], 1)

            def step(G, half, first):
                wait(act, full[3], 2 * (G - 1))
                for h in range(HG):
                    last = nc.scalar.activation(mag[:, half, h * HALF:(h + 1) * HALF], pos[:, :], ACT.Exp,
                                                scale=rate[:, bass.ds(G * HG + h, 1)])
                last.then_inc(mag_done, 1)
                wait(act, table, HG * G)
                act.wait_ge(reduced, G + 1)
                nc.scalar.activation(osc[:, :], ang[:, :], ACT.Sin, scale=TURN).then_inc(sine_done, 1)
                if not first:
                    evacuate(G - 1, 1 - half)

            loop(act, step, evacuate)

        @block.gpsimd
        def _(pool):
            def step(G, half, first):
                pool.wait_ge(sine_done, G + 1)
                pool.wait_ge(mag_done, G + 1)
                for h in range(HG):
                    s = slice(h * HALF, (h + 1) * HALF)
                    nc.gpsimd.tensor_tensor(mag[:, half, s], mag[:, half, s], osc[:, s], ALU.mult).then_inc(table, 1)
            loop(pool, step)

        @block.vector
        def _(dve):
            n = [0]
            L = lambda ins: link(dve, dve_step, n, ins)
            V = nc.vector
            for r in range(2):
                L(V.memset(role[64 * r:64 * r + 64, 0:1], 1.0 - 2.0 * r))
                L(V.memset(role[64 * r:64 * r + 64, 1:2], 0.25 * (1 - r)))
            dve.wait_ge(loaded, 48)
            L(V.tensor_scalar(growing[:, :], lam[:, 0:1], 0.0, None, ALU.is_gt))
            L(V.tensor_scalar(sgn[:, :], growing[:, :], -2.0, 1.0, ALU.mult, ALU.add))
            L(V.tensor_scalar(at[:, 0:1], sgn[:, :], 1.0, None, ALU.mult))
            L(V.tensor_scalar(at[:, 1:2], sgn[:, :], float(LK), None, ALU.mult))
            L(V.tensor_scalar(at[:, 2:3], growing[:, :], -float(HALF), None, ALU.mult))
            L(V.tensor_scalar(at[:, 3:4], growing[:, :], -float(HALF), float(HALF), ALU.mult, ALU.add))
            L(V.tensor_scalar(w[0][:, 0:1], growing[:, :], float(HALF - 1), None, ALU.mult))
            L(V.tensor_scalar(pos[:, :], t["ramp"][:, :], w[0][:, 0:1], None, ALU.subtract))
            dve.wait_ge(dt_exp, 1)
            d2 = dt[:, :].rearrange("p (h r) -> p r h", r=2)
            L(V.tensor_scalar(rate[:, :], d2[:, 0, :], lam[:, 0:1], None, ALU.mult))
            L(V.tensor_scalar(freq[:, :], d2[:, 1, :], lam[:, 1:2], None, ALU.mult))
            L(V.tensor_scalar(turns[:, :], freq[:, :], INV_TURN, None, ALU.mult))
            for k in range(4):
                L(V.tensor_scalar(ea[:, k, :], rate[:, :], at[:, k:k + 1], None, ALU.mult))
                L(V.tensor_scalar(aa[:, k, :], freq[:, :], at[:, k:k + 1], None, ALU.mult))
            for r, quarter in ((0, 0.25), (1, 0.0)):
                L(V.tensor_scalar(yy[:, r, :, :], aa[:, :, :], INV_TURN, quarter, ALU.mult, ALU.add))
            L(V.tensor_scalar(kk[:, :, :, :], yy[:, :, :, :], ROUND, ROUND, ALU.add, ALU.subtract))
            V.tensor_tensor(yy[:, :, :, :], yy[:, :, :, :], kk[:, :, :, :], ALU.subtract).then_inc(arg_ready, 1)
            dve.wait_ge(arg_done, 2)
            L(V.tensor_tensor(re[:, :, :], ea[:, :, :], yy[:, 0, :, :], ALU.mult))
            L(V.tensor_tensor(im[:, :, :], ea[:, :, :], yy[:, 1, :, :], ALU.mult))
            nr, dr, yr, yi, mg, rr, ri, qr, qi, tmp = (z[:, :] for z in w)
            lre, lim = lam[:, 0:1], lam[:, 1:2]
            ni, di = im[:, 0, :], im[:, 1, :]
            L(V.tensor_scalar(nr, re[:, 0, :], -1.0, None, ALU.add))
            L(V.tensor_scalar(dr, re[:, 1, :], -1.0, None, ALU.add))
            L(V.tensor_scalar(tmp, di, lim, None, ALU.mult))
            L(V.scalar_tensor_tensor(yr, dr, lre, tmp, ALU.mult, ALU.subtract))
            L(V.tensor_scalar(tmp, di, lre, None, ALU.mult))
            L(V.scalar_tensor_tensor(yi, dr, lim, tmp, ALU.mult, ALU.add))
            L(V.tensor_tensor(mg, yr, yr, ALU.mult))
            L(V.tensor_tensor(tmp, yi, yi, ALU.mult))
            L(V.scalar_tensor_tensor(mg, mg, EPS_TOK, tmp, ALU.add, ALU.add))
            L(V.reciprocal(mg, mg))
            L(V.tensor_tensor(rr, yr, mg, ALU.mult))
            L(V.scalar_tensor_tensor(ri, yi, -1.0, mg, ALU.mult, ALU.mult))
            L(V.tensor_tensor(qr, nr, rr, ALU.mult))
            L(V.tensor_tensor(tmp, ni, ri, ALU.mult))
            L(V.tensor_tensor(qr, qr, tmp, ALU.subtract))
            L(V.tensor_tensor(qi, nr, ri, ALU.mult))
            L(V.tensor_tensor(tmp, ni, rr, ALU.mult))
            L(V.tensor_tensor(qi, qi, tmp, ALU.add))
            for a in range(2):
                fr, fi = re[:, 2 + a, :], im[:, 2 + a, :]
                L(V.tensor_tensor(mg, qr, fr, ALU.mult))
                L(V.tensor_tensor(tmp, qi, fi, ALU.mult))
                L(V.tensor_tensor(mg, mg, tmp, ALU.subtract))
                L(V.tensor_scalar(gre[:, a, :], mg, role[:, 0:1], None, ALU.mult))
                L(V.tensor_tensor(mg, qr, fi, ALU.mult))
                L(V.tensor_tensor(tmp, qi, fr, ALU.mult))
                L(V.tensor_tensor(mg, mg, tmp, ALU.add))
                last = V.tensor_scalar(gim[:, a, :], mg, -1.0, None, ALU.mult)
                if a == 0:
                    L(last)
                else:
                    last.then_inc(params, 1)
            dve.wait_ge(params, 1)

            def evacuate(G, half):
                wait(dve, out_done[half], out_count(G, half))
                for h in range(1, HG, 2):
                    b = h % 4
                    dve.wait_ge(full[b], 2 * G + h // 4 + 1)
                    V.tensor_copy(res[:, half, h, :], kb[b][:, :]).then_inc(empty[b], 1)

            def step(G, half, first):
                wait(dve, w_turned, G - 1)
                dve.wait_ge(x_in[half], (G - half) * 8 + 16)
                src = xg[:, half, :].rearrange("c (h n r) -> c h n r", h=HG, r=2)
                for order in range(2):
                    for r in range(2):
                        last = V.tensor_scalar(xs[:, half, order, :, r, :], src[:, :, :, r ^ order], 1.0, None, ALU.mult)
                last.then_inc(swapped, 1)
                wait(dve, sine_done, G)
                for h in range(HG):
                    last = V.tensor_scalar(ang[:, h * HALF:(h + 1) * HALF], pos[:, :], turns[:, bass.ds(G * HG + h, 1)],
                                           role[:, 1:2], ALU.mult, ALU.add)
                last.then_inc(turned, 1)
                dve.wait_ge(turned, G + 1)
                V.tensor_scalar(near[:, :], ang[:, :], ROUND, ROUND, ALU.add, ALU.subtract).then_inc(rounded, 1)
                dve.wait_ge(rounded, G + 1)
                V.tensor_tensor(ang[:, :], ang[:, :], near[:, :], ALU.subtract).then_inc(reduced, 1)
                dve.wait_ge(w_turned, G + 1)
                wait(dve, full[3], 2 * (G - 1))
                va = wa[:, :].rearrange("p (h c) -> p h c", h=HG)
                vb = wb[:, :].rearrange("p (h c) -> p h c", h=HG)
                for a in range(2):
                    ga = gre[:, a, bass.ds(G * HG, HG)].unsqueeze(2).broadcast_to([P, HG, BATCH])
                    gb = gim[:, a, bass.ds(G * HG, HG)].unsqueeze(2).broadcast_to([P, HG, BATCH])
                    V.tensor_tensor(mm1[:, a, :, :], va, ga, ALU.mult)
                    last = V.tensor_tensor(mm2[:, a, :, :], vb, gb, ALU.mult)
                last.then_inc(w_read, 1)
                dve.wait_ge(w_read, G + 1)
                for a in range(2):
                    last = V.tensor_tensor(gw[:, half, :, a, :], mm1[:, a, :, :], mm2[:, a, :, :], ALU.add)
                last.then_inc(scaled, 1)
                dve.wait_ge(scaled, G + 1)
                if not first:
                    evacuate(G - 1, 1 - half)

            loop(dve, step, evacuate)

        @block.tensor
        def _(pe):
            ident = t["ident"]

            def products(G, half):
                for h in range(HG):
                    b = h % 4
                    if h == 0:
                        pe.wait_ge(scaled, G + 1)
                    pe.wait_ge(table, HG * G + h + 1)
                    wait(pe, empty[b], 2 * G + h // 4)
                    nc.tensor.matmul(kb[b][:, :], gw[:, half, h, :, :], mag[:, half, h * HALF:(h + 1) * HALF],
                                     start=True, stop=True).then_inc(full[b], 1)

            def step(G, half, first):
                pe.wait_ge(swapped, G + 1)
                wait(pe, w_read, G)
                for order, bank in ((0, wa), (1, wb)):
                    for h in range(HG):
                        last = nc.tensor.matmul(bank[:, h * BATCH:(h + 1) * BATCH],
                                                xs[:, half, order, h, :, :].rearrange("c r n -> c (r n)"),
                                                ident[0:BATCH, 0:BATCH], start=True, stop=True)
                last.then_inc(w_turned, 1)
                if not first:
                    products(G - 1, 1 - half)

            loop(pe, step, products)


def weight_codes(nc, dve, step, n, qw, part, word, wide, codes, planes):
    V = nc.vector
    U32 = mybir.dt.uint32
    for r in range(4):
        for k, plane in enumerate(planes):
            left = r < k
            link(dve, step, n, V.tensor_scalar(
                part[:, k, :].bitcast(U32), qw[:, plane, :, :].rearrange("p t w -> p (t w)").bitcast(U32), abs(r - k), 0x11111111 << k,
                ALU.logical_shift_left if left else ALU.logical_shift_right, ALU.bitwise_and))
        link(dve, step, n, V.tensor_tensor(part[:, 0:2, :], part[:, 0:2, :], part[:, 2:4, :], ALU.bitwise_or))
        link(dve, step, n, V.tensor_tensor(word[:, r, :], part[:, 0, :], part[:, 1, :], ALU.bitwise_or))
    for r in range(4):
        for j in range(8):
            last = V.tensor_scalar(wide[:, :, 4 * j + r].bitcast(U32), word[:, r, :].bitcast(U32), 4 * j, 15,
                                   ALU.logical_shift_right, ALU.bitwise_and)
    link(dve, step, n, last)
    link(dve, step, n, V.tensor_copy(codes[:, :], wide[:, :, :].rearrange("p a k -> p (a k)")))


MASKS = 4


def dense_weights(nc, t, dram):
    CODES = 16
    with ExitStack() as ctx:
        sb = lambda n, s, d=F32: ctx.enter_context(nc.sbuf_tensor(n, s, d))
        sem = lambda n: ctx.enter_context(nc.semaphore(n))
        qw = sb("q_qw", [P, 8, ND, 32], I32)
        part = sb("q_part", [P, 4, 256], I32)
        word = sb("q_word", [P, 4, 256], I32)
        wide = sb("q_wide", [P, 256, 32], I32)
        codes = sb("q_codes", [P, 256 * 32], BF16)
        lut = sb("q_lut", [P, ND * CODES])
        short = sb("q_short", [P, ND * CODES], BF16)
        lut_part = sb("q_lut_part", [P, 3, ND * CODES])
        lut_tile = sb("q_lut_tile", [P, 3, CODES])
        ident_bf = sb("q_ident_bf", [P, P], BF16)
        diagonal = sb("q_diagonal", [P, MASKS, 3, P], BF16)
        mask = sb("q_mask", [P, MASKS, DIM], BF16)
        w_rows = sb("q_w_rows", [P, DIM])
        w_ps = [ctx.enter_context(nc.psum_tensor(f"q_w_ps{i}", [P, 512], F32)) for i in range(2)]
        t_ps = [ctx.enter_context(nc.psum_tensor(f"q_t_ps{i}", [P, 512], F32)) for i in range(2)]
        loaded, dve_step = sem("q_loaded"), sem("q_dve_step")
        lut_ready, diagonal_done, mask_done, used = sem("q_lut_ready"), sem("q_diagonal_done"), sem("q_mask_done"), sem("q_used")
        rows_copied, turned, stored = sem("q_rows_copied"), sem("q_turned"), sem("q_stored")
        block = ctx.enter_context(nc.Block())

        def over_tiles(engine, tile):
            tile(0)
            with engine.Fori(1, ND) as o:
                tile(o)

        @block.sync
        def _(sp):
            sp.dma_start(qw[:, :, :, :], dram["qweight"].rearrange("b (t p) w -> p b t w", p=P)).then_inc(loaded, 16)
            sp.dma_start(lut[:, :].rearrange("p (t c) -> p t c", t=ND), dram["lut4"].rearrange("(t p) c -> p t c", p=P)).then_inc(loaded, 16)
            sp.wait_ge(loaded, 32)

        @block.vector
        def _(dve):
            n = [0]
            V = nc.vector
            dve.wait_ge(loaded, 32)
            for k in range(3):
                link(dve, dve_step, n, V.tensor_copy(short[:, :], lut[:, :]))
                link(dve, dve_step, n, V.tensor_copy(lut_part[:, k, :], short[:, :]))
                if k < 2:
                    link(dve, dve_step, n, V.tensor_tensor(lut[:, :], lut[:, :], lut_part[:, k, :], ALU.subtract))
            link(dve, dve_step, n, V.tensor_copy(ident_bf[:, :], t["ident"][:, :]))
            weight_codes(nc, dve, dve_step, n, qw, part, word, wide, codes, range(4))

            def store(o):
                wait(dve, turned, o + 1)
                for half in range(2):
                    last = V.tensor_scalar(t["w_low"][:, 4 * half:4 * half + 4, bass.ds(o * P, P)],
                                           t_ps[half][:, :].rearrange("p (i c) -> p i c", i=4), 1.0, None, ALU.mult)
                last.then_inc(stored, 1)

            def tile(o):
                wait(dve, diagonal_done, o * CODES)
                V.tensor_scalar(lut_tile[:, :, :], lut_part[:, :, bass.ds(o * CODES, CODES)], 1.0, None, ALU.mult).then_inc(lut_ready, 1)
                for c in range(CODES):
                    wait(dve, used, o * CODES + c - (MASKS - 1))
                    V.tensor_scalar(mask[:, c % MASKS, :], codes[:, bass.ds(o * DIM, DIM)], float(c), None,
                                    ALU.is_equal).then_inc(mask_done, 1)
                    if c == MASKS - 1 and not (isinstance(o, int) and o == 0):
                        store(o - 1)
                wait(dve, used, o * CODES + CODES)
                for half in range(2):
                    V.tensor_scalar(w_rows[:, 512 * half:512 * half + 512], w_ps[half][:, :], 1.0, None, ALU.mult).then_inc(rows_copied, 1)

            over_tiles(dve, tile)
            store(ND - 1)

        @block.scalar
        def _(act):
            def tile(o):
                wait(act, lut_ready, o + 1)
                for c in range(CODES):
                    wait(act, used, o * CODES + c - (MASKS - 1))
                    for k in range(3):
                        last = nc.scalar.activation(diagonal[:, c % MASKS, k, :], ident_bf[:, :], ACT.Copy,
                                                    scale=lut_tile[:, k, c:c + 1])
                    last.then_inc(diagonal_done, 1)

            over_tiles(act, tile)

        @block.tensor
        def _(pe):
            def tile(o):
                wait(pe, rows_copied, o * 2)
                for c in range(CODES):
                    wait(pe, mask_done, o * CODES + c + 1)
                    wait(pe, diagonal_done, o * CODES + c + 1)
                    for k in range(3):
                        for half in range(2):
                            last = nc.tensor.matmul(w_ps[half][:, :], diagonal[:, c % MASKS, k, :],
                                                    mask[:, c % MASKS, 512 * half:512 * half + 512],
                                                    start=(c == 0 and k == 0), stop=(c == CODES - 1 and k == 2))
                    last.then_inc(used, 1)
                wait(pe, rows_copied, o * 2 + 2)
                wait(pe, stored, o)
                for i in range(ND):
                    last = nc.tensor.transpose(t_ps[i // 4][:, P * (i % 4):P * (i % 4) + P], w_rows[:, P * i:P * i + P], t["ident"][:, :])
                last.then_inc(turned, 1)

            over_tiles(pe, tile)


PE_PLAN = {0: [("ffn_late", (4, 4, 8))], 2: [("add", 0), ("ffn_late", (5, 0, 4))], 3: [("add", 1), ("ffn_late", (5, 4, 8))],
           4: [("add", 2), ("ffn_late", (6, 0, 4))], 5: [("add", 3), ("ffn_late", (6, 4, 8))],
           6: [("out_low", 0)], 7: [("out_low", 1), ("ffn_late", (7, 0, 4))], 8: [("turn1", 0), ("ffn_late", (7, 4, 8))],
           9: [("turn1", 1)], 10: [("turn1", 2)], 11: [("turn1", 3)],
           12: [("xproj", (0, 3))], 13: [("xproj", (3, 6))], 14: [("turn2", 0), ("xproj", (6, 8))],
           15: [("turn2", 1)], 16: [("turn2", 2), ("dt", 0)], 17: [("turn2", 3)], 18: [("dt", 1), ("out_high", 0)],
           19: [("out_high", 1), ("ffn", (0, 0, 4))], 20: [("dt", 2), ("ffn", (0, 4, 8))],
           22: [("dt", 3), ("ffn", (1, 0, 4))], 23: [("ffn", (1, 4, 8))],
           25: [("ffn", (2, 0, 4))], 26: [("ffn", (2, 4, 8))], 28: [("ffn", (3, 0, 4))], 29: [("ffn", (3, 4, 8))],
           31: [("ffn", (4, 0, 4))]}
ACT_PLAN = {1: [("ffn_late", 4)], 4: [("ffn_late", 5), ("root1", 0)], 6: [("norm1", 0)], 7: [("ffn_late", 6), ("norm1", 1)],
            9: [("root2", 0), ("turn1", 0)], 10: [("turn1", 1), ("ffn_late", 7)], 11: [("turn1", 2)],
            12: [("turn1", 3)], 13: [("norm2", 0)], 14: [("norm2", 1)], 15: [("turn2", 0)], 16: [("xproj", 0), ("turn2", 1)],
            17: [("turn2", 2), ("dt", 0)], 18: [("turn2", 3)], 19: [("dt", 1)], 20: [("soft", (0, 0))],
            21: [("dt", 2), ("soft", (0, 1))], 22: [("ffn", 0), ("soft", (0, 2))], 24: [("dt", 3), ("soft", (1, 0))],
            25: [("ffn", 1), ("soft", (1, 1))], 26: [("soft", (1, 2))], 28: [("ffn", 2)], 31: [("ffn", 3)]}
DVE_PLAN = {0: [("stats1", 0)], 1: [("last_block", 0)], 2: [("stats1", 1)], 3: [("add", 0)], 4: [("add", 1), ("newton1", 0)],
            5: [("add", 2)], 6: [("add", 3), ("stats2", 0)], 7: [("out_low", 0), ("stats2", 1)], 8: [("out_low", 1)],
            10: [("newton2", 0)], 19: [("out_high", 0)], 20: [("out_high", 1)], 24: [("dt", 0)], 27: [("dt", 1)]}
POOL_PLAN = {29: [("u", 0)], 30: [("u", 1)], 31: [("u", 2), ("u", 3), ("reset", 0)]}
LN_VAR = 6
LN_STEPS = {1: LN_VAR + 5, 2: LN_VAR + 8}
PREPARE = {"root1", "stats1", "newton1", "norm1", "turn1", "xproj", "dt", "soft", "u", "reset"}
LATE = {"ffn_late", "out_low", "out_high"}
P_USES = 1 + ND // 2
X_GROUPS = {"add": 4, "out_low": 2, "turn1": 4, "turn2": 4, "out_high": 2}
X_STEP = sum(X_GROUPS.values()) // 2
RING = 8


def x_start(u):
    return X_STEP * (u - 2) + (X_GROUPS["turn1"] * 3 + X_GROUPS["add"] + X_GROUPS["turn2"]) // 2


FIRST_ENTRIES = [(-1, 0, ["turn1"]), (0, 2, ["turn1"]), (1, 4, ["add", "turn1", "turn2"]), (2, x_start(2), list(X_GROUPS))]
NO_PREPARATION = ["add", "out_low", "turn2", "out_high"]
LAST_ENTRIES = [(BATCH - 1, x_start(BATCH - 1), NO_PREPARATION), (BATCH, x_start(BATCH - 1) + 6, NO_PREPARATION),
                (BATCH + 1, x_start(BATCH - 1) + 12, ["out_low", "out_high"])]

class Exchange:

    def __init__(self, start, groups=tuple(X_GROUPS)):
        self.start, self.first, k = start, {}, 0
        for name, size in X_GROUPS.items():
            if name in groups:
                self.first[name] = k
                k += size

    def use(self, name, r):
        k = self.first[name] + r
        return k % 2, self.start + k // 2


def scan_pass(nc, t, dram, mixed, before, rows_bc, out):
    with ExitStack() as ctx:
        sb = lambda n, s, d=F32: ctx.enter_context(nc.sbuf_tensor(n, s, d))
        sem = lambda n: ctx.enter_context(nc.semaphore(n))
        h_in = sb("s_h_in", [P, 2, DIM])
        h1 = sb("s_h1", [P, 2, 2, DIM])
        xn = sb("s_xn", [P, 2, DIM])
        x_t = sb("s_x_t", [P, 2, ND, LEN])
        x2_t = sb("s_x2_t", [P, ND, LEN])
        y_t = sb("s_y_t", [P, ND, LEN])
        dt_t = sb("s_dt_t", [P, 2, ND, LEN])
        u_t = sb("s_u_t", [P, 2, ND, LEN])
        bc = sb("s_bc", [P, 2, 2 * NS, LEN])
        xp = sb("s_xp", [RANK + 2 * NS, LEN])
        ring = sb("s_ring", [P, RING, CW])
        stats = sb("s_stats", [P, 2, 2, 6])
        large = sb("s_large", [P, ND, 1])
        nudge = sb("s_nudge", [P, 1])
        small = {which: [sb(f"s_small{which}_{i}", [P, 2]) for i in range(8)] for which in (1, 2)}
        decay = [ctx.enter_context(nc.psum_tensor("s_decay0", [P, 1024], F32))[:, 0:CW], sb("s_decay1", [P, CW])[:, :]]
        y_ps = [ctx.enter_context(nc.psum_tensor(f"s_y_ps{i}", [P, 512], F32)) for i in range(2)]
        p_ps = ctx.enter_context(nc.psum_tensor("s_p_ps", [P, 512], F32))
        f_ps = ctx.enter_context(nc.psum_tensor("s_f_ps", [P, 512], F32))
        xch = [ctx.enter_context(nc.psum_tensor(f"s_xch{i}", [P, 512], F32)) for i in range(2)]

        decay_done, dbx_done, scan_done, hc_done, sum_done = (
            sem("s_decay_done"), sem("s_dbx_done"), sem("s_scan_done"), sem("s_hc_done"), sem("s_sum_done"))
        y_done = sem("s_y_done")
        x_full = [sem(f"s_x_full{i}") for i in range(2)]
        x_empty = [sem(f"s_x_empty{i}") for i in range(2)]
        f_full, f_empty = sem("s_f_full"), sem("s_f_empty")
        p_full, p_empty = sem("s_p_full"), sem("s_p_empty")
        ln_step = {1: sem("s_ln1_step"), 2: sem("s_ln2_step")}
        root = {1: sem("s_root1"), 2: sem("s_root2")}
        norm_done = {1: sem("s_norm1"), 2: sem("s_norm2")}
        spread_out, large_set = sem("s_spread_out"), sem("s_large_set")
        bc_in = [sem(f"s_bc_in{i}") for i in range(2)]
        soft_step, dt_done, u_done, reset_done = sem("s_soft_step"), sem("s_dt_done"), sem("s_u_done"), sem("s_reset_done")
        loaded = sem("s_loaded")
        rows_in = [sem(f"s_rows_in{i}") for i in range(2)]
        kept = [sem(f"s_kept{i}") for i in range(2)]
        stored = [sem(f"s_stored{i}") for i in range(2)]
        block = ctx.enter_context(nc.Block())

        def rows(k):
            return HEADS if k == 0 else TXT

        def cols(k):
            return slice(0, HEADS) if k == 0 else slice(HEADS, LEN)

        def run(engine, chunk, stages, plan, stages_first=False):
            def entry(u, par, x, groups, scan=True):
                for s in range(CHUNKS):
                    if scan and not stages_first:
                        chunk(u, par, s)
                    for name, arg in plan.get(s, []):
                        if name in PREPARE:
                            if "turn1" in groups:
                                stages[name](u + 1, 1 - par, arg, x)
                        elif name in LATE:
                            if "out_low" in groups:
                                stages[name](u - 2, par, arg, x)
                        elif "add" in groups:
                            stages[name](u - 1, 1 - par, arg, x)
                    if scan and stages_first:
                        chunk(u, par, s)

            for u, start, groups in FIRST_ENTRIES:
                entry(u, u % 2, Exchange(start, groups), groups, scan=u >= 0)
            with engine.Fori(0, (BATCH - 4) // 2) as i:
                entry(i * 2 + 3, 1, Exchange(i * (2 * X_STEP) + x_start(3)), X_GROUPS)
                entry(i * 2 + 4, 0, Exchange(i * (2 * X_STEP) + x_start(4)), X_GROUPS)
            for u, start, groups in LAST_ENTRIES:
                entry(u, u % 2, Exchange(start, groups), groups, scan=u < BATCH)

        @block.sync
        def _(sp):
            def rows_of(target, v, signal):
                sp.dma_start(target[:, 0, :], mixed[bass.ds(v, 1), :, :].rearrange("a p l -> (a p) l")).then_inc(signal, 16)
                sp.dma_start(target[0:TXT, 1, :], dram["txt"][bass.ds(v, 1), :, :].rearrange("a p l -> (a p) l")).then_inc(signal, 16)

            def load(v):
                wait(sp, norm_done[1], v * 2)
                rows_of(h_in, v, loaded)

            def load_rows(v, par):
                wait(sp, stored[par], (v - par) * 16)
                rows_of(h1[:, par, :, :], v, rows_in[par])

            def save(v, par, target, signal):
                for k in range(2):
                    sp.dma_start(target[bass.ds(v, 1), cols(k), :].rearrange("a p l -> (a p) l"),
                                 h1[0:rows(k), par, k, :]).then_inc(signal, 16)

            def keep(v, par, x):
                for r in (2, 3):
                    b, c = x.use("add", r)
                    wait(sp, x_empty[b], c + 1)
                save(v, par, before, kept[par])

            def write(v, par, x):
                for r in (0, 1):
                    b, c = x.use("out_high", r)
                    wait(sp, x_empty[b], c + 1)
                save(v, par, out, stored[par])

            def spread(v, par):
                wait(sp, p_empty, v * P_USES + 1)
                sp.dma_start(rows_bc[par:par + 1, :, :].rearrange("a n l -> (a n) l"), xp[RANK:, :]).then_inc(spread_out, 16)
                wait(sp, spread_out, v * 16 + 16)
                for k in range(2):
                    sp.dma_start(bc[:, par, NS * k:NS * k + NS, :],
                                 rows_bc[par:par + 1, NS * k:NS * k + NS, :].broadcast_to([P, NS, LEN])).then_inc(bc_in[par], 16)

            def entry(u, par, x, groups, ahead=True):
                if "add" in groups:
                    keep(u - 1, 1 - par, x)
                if "turn1" in groups:
                    if ahead:
                        load(u + 2)
                    spread(u + 1, 1 - par)
                if "out_low" in groups:
                    write(u - 2, par, x)
                if not isinstance(u, int) or 0 <= u < BATCH:
                    load_rows(u, par)

            rows_of(h_in, 0, loaded)
            for u, start, groups in FIRST_ENTRIES:
                entry(u, u % 2, Exchange(start, groups), groups)
            with sp.Fori(0, (BATCH - 6) // 2) as i:
                entry(i * 2 + 3, 1, Exchange(i * (2 * X_STEP) + x_start(3)), X_GROUPS)
                entry(i * 2 + 4, 0, Exchange(i * (2 * X_STEP) + x_start(4)), X_GROUPS)
            for u in (BATCH - 3, BATCH - 2):
                entry(u, u % 2, Exchange(x_start(u)), X_GROUPS, ahead=u + 2 < BATCH)
            for u, start, groups in LAST_ENTRIES:
                entry(u, u % 2, Exchange(start, groups), groups)
            for i in range(2):
                sp.wait_ge(kept[i], 32 * BATCH // 2)
                sp.wait_ge(stored[i], 32 * BATCH // 2)

        @block.tensor
        def _(pe):
            ident = t["ident"]

            def claim(x, name, r):
                b, c = x.use(name, r)
                wait(pe, x_empty[b], c)
                return xch[b], x_full[b]

            def emptied(x, name):
                for r in (2, 3):
                    b, c = x.use(name, r)
                    wait(pe, x_empty[b], c + 1)

            def chunk(u, par, s):
                if s:
                    sums(u, s - 1)
                if s == CHUNKS - 1:
                    sums(u, s)

            def sums(u, s):
                j = s // 4
                wait(pe, hc_done, u * CHUNKS + s + 1)
                if s % 4 == 0:
                    wait(pe, y_done, u * ND + j - 1)
                for n in range(CN):
                    last = nc.tensor.matmul(y_ps[j % 2][:, 0:LEN], ident[:, :], ring[:, s % RING, n * LEN:(n + 1) * LEN],
                                            start=(s % 4 == 0 and n == 0), stop=(s % 4 == 3 and n == CN - 1))
                last.then_inc(sum_done, 1)

            def add(v, par, r, x):
                k, side = r // 2, r % 2
                bank, full = claim(x, "add", r)
                wait(pe, y_done, v * ND + ND)
                for j in range(4):
                    last = nc.tensor.transpose(bank[0:rows(k), P * j:P * j + P], x_t[:, par, 4 * side + j, cols(k)], ident[:, :])
                last.then_inc(full, 1)

            def turn(which, v, r, x):
                bank, full = claim(x, f"turn{which}", r)
                wait(pe, norm_done[which], v * 2 + 2)
                for j in range(2):
                    for k in range(2):
                        last = nc.tensor.transpose(bank[:, LEN * j + cols(k).start:LEN * j + cols(k).stop],
                                                   xn[0:rows(k), k, P * (2 * r + j):P * (2 * r + j) + P],
                                                   ident[0:rows(k), 0:rows(k)])
                last.then_inc(full, 1)

            def ffn(v, par, piece, x):
                o, first, end = piece
                if first == 0:
                    wait(pe, f_empty, v * ND + o)
                    if o == 0:
                        emptied(x, "turn2")
                for i in range(first, end):
                    last = nc.tensor.matmul(f_ps[:, 0:LEN], t["w_low"][:, i, P * o:P * o + P], x2_t[:, i, :],
                                            start=(i == 0), stop=(i == ND - 1))
                if end == ND:
                    last.then_inc(f_full, 1)

            def finish(name, v, k, x):
                side = ("out_low", "out_high").index(name)
                bank, full = claim(x, name, k)
                wait(pe, f_empty, v * ND + 4 * side + 4)
                for j in range(4):
                    last = nc.tensor.transpose(bank[0:rows(k), P * j:P * j + P], y_t[:, 4 * side + j, cols(k)], ident[:, :])
                last.then_inc(full, 1)

            def xproj(v, par, piece, x):
                first, end = piece
                if first == 0:
                    wait(pe, p_empty, v * P_USES)
                    emptied(x, "turn1")
                for i in range(first, end):
                    last = nc.tensor.matmul(p_ps[0:RANK + 2 * NS, 0:LEN], t["xpw_t"][:, i, :], x_t[:, par, i, :],
                                            start=(i == 0), stop=(i == ND - 1))
                if end == ND:
                    last.then_inc(p_full, 1)

            def dt_proj(v, par, r, x):
                wait(pe, p_empty, v * P_USES + r + 1)
                for k in range(2):
                    j = 2 * r + k
                    last = nc.tensor.matmul(p_ps[:, LEN * k:LEN * k + LEN], t["dtw_t"][:, P * j:P * j + P],
                                            xp[0:RANK, :], start=True, stop=True)
                last.then_inc(p_full, 1)

            stages = {"add": add, "ffn": ffn, "ffn_late": ffn, "xproj": xproj, "dt": dt_proj,
                      "out_low": lambda v, par, k, x: finish("out_low", v, k, x),
                      "out_high": lambda v, par, k, x: finish("out_high", v, k, x),
                      "turn2": lambda v, par, r, x: turn(2, v, r, x), "turn1": lambda v, par, r, x: turn(1, v, r, x)}
            run(pe, chunk, stages, PE_PLAN, stages_first=True)

        @block.scalar
        def _(act):
            A = nc.scalar
            act.add_instruction(mybir.InstLoadActFuncSet(name=nc.get_next_instruction_name(), act_func_set_id=LN_EXP_TABLES))

            def take(x, name, r):
                b, c = x.use(name, r)
                wait(act, x_full[b], c + 1)
                return xch[b], x_empty[b]

            def chunk(u, par, s):
                j, n0 = s // 4, CN * (s % 4)
                wait(act, scan_done, u * CHUNKS + s - 1)
                if s == 0:
                    wait(act, reset_done, u + 1)
                for n in range(CN):
                    last = A.activation(decay[s % 2][:, n * LEN:(n + 1) * LEN], dt_t[:, par, j, :], ACT.Exp,
                                        scale=t["a_neg"][:, j, n0 + n:n0 + n + 1])
                last.then_inc(decay_done, 1)

            def roots(which, v):
                w = small[which]
                wait(act, ln_step[which], v * LN_STEPS[which] + LN_VAR)
                A.activation(w[1][:, :], w[0][:, :], ACT.Ln).then_inc(root[which], 1)
                wait(act, root[which], v * 2 + 1)
                A.activation(w[2][:, :], w[1][:, :], ACT.Exp, scale=-0.5).then_inc(root[which], 1)

            def turn2(v, par, r, x):
                bank, empty = take(x, "turn2", r)
                A.activation(x2_t[:, 2 * r:2 * r + 2, :], bank[:, 0:2 * LEN].rearrange("p (j l) -> p j l", j=2),
                             ACT.Copy).then_inc(empty, 1)

            def turn1(v, par, r, x):
                bank, empty = take(x, "turn1", r)
                A.activation(x_t[:, par, 2 * r:2 * r + 2, :], bank[:, 0:2 * LEN].rearrange("p (j l) -> p j l", j=2),
                             ACT.Copy).then_inc(empty, 1)

            def norm(which, v, par, k):
                src, rstd, shift = (h_in if which == 1 else h1[:, par, :, :]), small[which][6], small[which][7]
                n = rows(k)
                if k == 0:
                    wait(act, ln_step[which], v * LN_STEPS[which] + LN_VAR + 5)
                A.activation(xn[0:n, k, :], src[0:n, k, :], ACT.Identity, scale=rstd[0:n, k:k + 1],
                             bias=shift[0:n, k:k + 1]).then_inc(norm_done[which], 1)

            def ffn(v, par, o, x):
                wait(act, f_full, v * ND + o + 1)
                A.activation(y_t[:, o, :], f_ps[:, 0:LEN], ACT.Identity, bias=t["y_bias"][:, o:o + 1]).then_inc(f_empty, 1)

            def xproj(v, par, r, x):
                wait(act, p_full, v * P_USES + 1)
                wait(act, spread_out, v * 16)
                A.activation(xp[:, :], p_ps[0:RANK + 2 * NS, 0:LEN], ACT.Copy).then_inc(p_empty, 1)

            def dt_bias(v, par, r, x):
                wait(act, p_full, v * P_USES + r + 2)
                for k in range(2):
                    j = 2 * r + k
                    last = A.activation(u_t[:, par, j, :], p_ps[:, LEN * k:LEN * k + LEN], ACT.Identity,
                                        bias=t["dt_bias"][:, j:j + 1])
                last.then_inc(p_empty, 1)

            def soft(v, par, piece, x):
                half, step = piece
                d, z = dt_t[:, par, 4 * half:4 * half + 4, :], u_t[:, par, 4 * half:4 * half + 4, :]
                if step == 0:
                    wait(act, p_empty, v * P_USES + 2 * half + 3)
                    A.activation(d, z, ACT.Abs).then_inc(soft_step, 1)
                else:
                    wait(act, soft_step, v * 6 + 3 * half + step)
                    if step == 1:
                        A.activation(d, d, ACT.Exp, scale=-1.0).then_inc(soft_step, 1)
                    else:
                        A.activation(d, d, ACT.Ln, bias=1.0).then_inc(soft_step, 1)

            stages = {"turn2": turn2, "turn1": turn1, "ffn": ffn, "ffn_late": ffn, "xproj": xproj, "dt": dt_bias, "soft": soft,
                      "root2": lambda v, *_: roots(2, v), "root1": lambda v, *_: roots(1, v),
                      "norm2": lambda v, par, k, *_: norm(2, v, par, k), "norm1": lambda v, par, k, *_: norm(1, v, par, k)}
            run(act, chunk, stages, ACT_PLAN)

        @block.gpsimd
        def _(pool):
            def chunk(u, par, s):
                j, n0 = s // 4, CN * (s % 4)
                if s == 0:
                    wait(pool, u_done, u * 4 + 4)
                    wait(pool, bc_in[par], (u - par) * 16 + 32)
                wait(pool, sum_done, u * CHUNKS + s - (RING - 1))
                nc.gpsimd.tensor_tensor(ring[:, s % RING, :].rearrange("p (n l) -> p n l", n=CN), bc[:, par, n0:n0 + CN, :],
                                        u_t[:, par, j, :].unsqueeze(1).broadcast_to([P, CN, LEN]), ALU.mult).then_inc(dbx_done, 1)

            def scaled_input(v, par, r, x):
                if r % 2 == 0:
                    wait(pool, dt_done, v * 2 + r // 2 + 1)
                nc.gpsimd.tensor_tensor(u_t[:, par, 2 * r:2 * r + 2, :], dt_t[:, par, 2 * r:2 * r + 2, :],
                                        x_t[:, par, 2 * r:2 * r + 2, :], ALU.mult).then_inc(u_done, 1)

            def reset(v, par, r, x):
                wait(pool, u_done, v * 4 + 4)
                nc.gpsimd.tensor_tensor(dt_t[:, par, :, 0:1], dt_t[:, par, :, 0:1], large[:, :, :], ALU.add).then_inc(reset_done, 1)

            nc.gpsimd.memset(large[:, :, :], RESET_DT).then_inc(large_set, 1)
            pool.wait_ge(large_set, 1)
            run(pool, chunk, {"u": scaled_input, "reset": reset}, POOL_PLAN)

        @block.vector
        def _(dve):
            V = nc.vector

            def take(x, name, r):
                b, c = x.use(name, r)
                wait(dve, x_full[b], c + 1)
                return xch[b], x_empty[b]

            def block_output(u, par, j):
                wait(dve, sum_done, u * CHUNKS + 4 * j + 4)
                V.scalar_tensor_tensor(x_t[:, par, j, :], x_t[:, par, j, :], t["d_col"][:, j:j + 1], y_ps[j % 2][:, 0:LEN],
                                       ALU.mult, ALU.add).then_inc(y_done, 1)

            def scan(u, par, s):
                g = u * CHUNKS + s
                wait(dve, decay_done, g + 1)
                wait(dve, dbx_done, g + 1)
                V.tensor_tensor_scan(out=ring[:, s % RING, :], data0=decay[s % 2], data1=ring[:, s % RING, :],
                                     initial=0.0, op0=ALU.mult, op1=ALU.add).then_inc(scan_done, 1)

            def times_c(u, par, s):
                n0 = CN * (s % 4)
                wait(dve, scan_done, u * CHUNKS + s + 1)
                V.tensor_tensor(ring[:, s % RING, :], ring[:, s % RING, :],
                                bc[:, par, NS + n0:NS + n0 + CN, :].rearrange("p n l -> p (n l)"), ALU.mult).then_inc(hc_done, 1)

            def chunk(u, par, s):
                scan(u, par, s)
                if s:
                    times_c(u, par, s - 1)
                if s == CHUNKS - 1:
                    times_c(u, par, s)
                if s % 4 == 1 and s > 1:
                    block_output(u, par, s // 4 - 1)

            def add(v, par, r, x):
                k, side = r // 2, r % 2
                bank, empty = take(x, "add", r)
                if r == 0:
                    wait(dve, rows_in[par], (v - par) * 16 + 32)
                V.tensor_tensor(h1[0:rows(k), par, k, 512 * side:512 * side + 512], bank[0:rows(k), :],
                                h1[0:rows(k), par, k, 512 * side:512 * side + 512], ALU.add).then_inc(empty, 1)

            def ln_stats(which, v, par, tile, x):
                src, mv, step = (h_in if which == 1 else h1[:, par, :, :]), t[f"mv{which}"], ln_step[which]
                ve, base, n = small[which][0], v * LN_STEPS[which] + 3 * tile, rows(tile)
                if which == 1:
                    if tile == 0:
                        wait(dve, loaded, v * 32 + 32)
                else:
                    for k in (0, 1):
                        b, c = x.use("add", 2 * tile + k)
                        wait(dve, x_empty[b], c + 1)
                for i in range(2):
                    last = V.bn_stats(stats[0:n, tile, i, :], src[0:n, tile, 512 * i:512 * i + 512])
                last.then_inc(step, 1)
                wait(dve, step, base + 1)
                V.memset(nudge[:, :], 0.0)
                V.bn_aggr(mv[0:n, tile, :], stats[0:n, tile, :, :].rearrange("p a b -> p (a b)")).then_inc(step, 1)
                wait(dve, step, base + 2)
                V.tensor_scalar(ve[:, tile:tile + 1], mv[:, tile, 1:2], EPS_LN, None, ALU.add).then_inc(step, 1)

            def newton(which, v):
                ve, _, r0, sq, pr, co, rstd, shift = (z[:, :] for z in small[which])
                step, base = ln_step[which], v * LN_STEPS[which] + LN_VAR
                wait(dve, root[which], v * 2 + 2)
                wait(dve, step, base)
                V.tensor_tensor(sq, r0, r0, ALU.mult).then_inc(step, 1)
                wait(dve, step, base + 1)
                V.tensor_tensor(pr, sq, ve, ALU.mult).then_inc(step, 1)
                wait(dve, step, base + 2)
                V.tensor_scalar(co, pr, -0.5, 1.5, ALU.mult, ALU.add).then_inc(step, 1)
                wait(dve, step, base + 3)
                V.tensor_tensor(rstd, co, r0, ALU.mult).then_inc(step, 1)
                wait(dve, step, base + 4)
                V.scalar_tensor_tensor(shift, t[f"mv{which}"][:, :, 0], -1.0, rstd, ALU.mult, ALU.mult).then_inc(step, 1)
                if which == 2:
                    row_norms(v)

            def row_norms(v):
                sq, pr, rstd = small[2][3], small[2][4], small[2][6]
                step, base = ln_step[2], v * LN_STEPS[2] + LN_VAR + 5
                V.tensor_tensor(sq[:, :], rstd[:, :], rstd[:, :], ALU.mult).then_inc(step, 1)
                wait(dve, step, base + 1)
                V.tensor_tensor(pr[:, :], sq[:, :], t["mv2"][:, :, 1], ALU.mult).then_inc(step, 1)
                wait(dve, step, base + 2)
                V.scalar_tensor_tensor(t["over"][:, :], pr[:, :], float(DIM), t["over"][:, :], ALU.mult, ALU.max).then_inc(step, 1)

            def dt_total(v, par, half, x):
                wait(dve, soft_step, v * 6 + 3 * half + 3)
                d, z = (a[:, par, 4 * half:4 * half + 4, :].rearrange("p j l -> p (j l)") for a in (dt_t, u_t))
                V.scalar_tensor_tensor(d, z, 0.0, d, ALU.max, ALU.add).then_inc(dt_done, 1)

            def finish(name, v, par, k, x):
                side = ("out_low", "out_high").index(name)
                bank, empty = take(x, name, k)
                if side == 0 and k == 0:
                    wait(dve, kept[par], (v - par) * 16 + 32)
                V.tensor_tensor(h1[0:rows(k), par, k, 512 * side:512 * side + 512], bank[0:rows(k), :],
                                h1[0:rows(k), par, k, 512 * side:512 * side + 512], ALU.add).then_inc(empty, 1)

            stages = {"add": add, "dt": dt_total, "last_block": lambda v, par, *_: block_output(v, par, ND - 1),
                      "out_low": lambda v, par, k, x: finish("out_low", v, par, k, x),
                      "out_high": lambda v, par, k, x: finish("out_high", v, par, k, x),
                      "stats1": lambda v, par, k, x: ln_stats(1, v, par, k, x),
                      "stats2": lambda v, par, k, x: ln_stats(2, v, par, k, x),
                      "newton1": lambda v, *_: newton(1, v), "newton2": lambda v, *_: newton(2, v)}
            run(dve, chunk, stages, DVE_PLAN)


def general_path(nc, t, dram, kept, before, out):
    any_over(nc, t)
    with ExitStack() as ctx:
        general_weights(nc, t, dram, kept, t["flag"], ctx)
        general_rows(nc, t, t["flag"], before, out)


def any_over(nc, t):
    with ExitStack() as ctx:
        sb = lambda n, s, d=F32: ctx.enter_context(nc.sbuf_tensor(n, s, d))
        pb = lambda n, s: ctx.enter_context(nc.psum_tensor(n, s, F32))
        sem = lambda n: ctx.enter_context(nc.semaphore(n))
        seen = sb("g_seen", [P, 2])
        ones = sb("g_ones", [P, 1])
        count = sb("g_count", [1, 1])
        count_ps = pb("g_count_ps", [P, 512])
        step, counted = sem("g_step"), sem("g_counted")
        block = ctx.enter_context(nc.Block())

        @block.vector
        def _(dve):
            n = [0]
            V = nc.vector
            V.memset(ones[:, :], 1.0)
            V.tensor_scalar(seen[:, :], t["over"][:, :], NORM_LIMIT * NORM_LIMIT, None, ALU.is_gt).then_inc(step, 1)
            dve.wait_ge(counted, 1)
            n[0] = 1
            link(dve, step, n, V.reduce_sum(count[:, :], count_ps[0:1, 0:2], mybir.AxisListType.X))
            link(dve, step, n, V.tensor_copy(t["flag"][:, :], count[:, :]))

        @block.tensor
        def _(pe):
            pe.wait_ge(step, 1)
            nc.tensor.matmul(count_ps[0:1, 0:2], ones[:, :], seen[:, :], start=True, stop=True).then_inc(counted, 1)



def general_weights(nc, t, dram, kept, flag, outer):
    t["w_high"] = outer.enter_context(nc.sbuf_tensor("w_high", [P, ND, DIM], F32))
    with ExitStack() as ctx:
        sb = lambda n, s, d=F32: ctx.enter_context(nc.sbuf_tensor(n, s, d))
        pb = lambda n, s: ctx.enter_context(nc.psum_tensor(n, s, F32))
        sem = lambda n: ctx.enter_context(nc.semaphore(n))
        qw = sb("h_qw", [P, 8, ND, 32], I32)
        part = sb("h_part", [P, 4, 256], I32)
        word = sb("h_word", [P, 4, 256], I32)
        wide = sb("h_wide", [P, 256, 32], I32)
        codes = [sb(f"h_codes{i}", [P, 256 * 32], BF16) for i in range(2)]
        tables = sb("h_tables", [P, P, 16])
        repeat = sb("h_repeat", [P, 16 * P], BF16)
        square = sb("h_square", [P, 8, 16])
        hot = [sb(f"h_hot{i}", [P, DIM]) for i in range(2)]
        picked = sb("h_picked", [P, DIM])
        rep = [pb(f"h_rep{i}", [P, DIM]) for i in range(2)]
        row_ps = pb("h_row_ps", [P, DIM])
        sum_ps = pb("h_sum_ps", [P, 512])
        loaded, dve_step, ready = sem("h_loaded"), sem("h_dve_step"), sem("h_ready")
        repeated, hot_done, rowed, picked_done, summed, stored = (
            sem("h_repeated"), sem("h_hot_done"), sem("h_rowed"), sem("h_picked_done"), sem("h_summed"), sem("h_stored"))
        block = ctx.enter_context(nc.Block())

        @block.sync
        def _(sp):
            go = sp.value_load(flag[0:1, 0:1])
            with sp.If(go != 0):
                sp.dma_start(qw[:, :, :, :], dram["qweight"].rearrange("b (t p) w -> p b t w", p=P)).then_inc(loaded, 16)
                for o in range(8):
                    sp.dma_start(tables[16 * o:16 * o + 16, :, :],
                                 dram["lut8"].rearrange("(g o) (a b) -> o a g b", o=8, a=16)[o]).then_inc(loaded, 16)
                sp.dma_start(repeat[:, :], kept["spread"]).then_inc(loaded, 16)
                sp.wait_ge(loaded, 160)

        @block.vector
        def _(dve):
            V = nc.vector
            go = dve.value_load(flag[0:1, 0:1])
            with dve.If(go != 0):
                n = [0]
                dve.wait_ge(loaded, 160)
                for i in range(2):
                    weight_codes(nc, dve, dve_step, n, qw, part, word, wide, codes[i], range(4 * i, 4 * i + 4))
                V.memset(part[:, 0, 0:1], 0).then_inc(ready, 1)
                V.memset(part[:, 1, 0:1], 0).then_inc(stored, 1)
                with dve.Fori(0, ND) as o:
                    for j in range(16):
                        g = o * 16 + j
                        dve.wait_ge(repeated, g + 1)
                        for i in range(2):
                            V.tensor_scalar(hot[i][:, :], rep[i][:, :], t["code_col"][:, 0:1], None, ALU.is_equal)
                        V.tensor_tensor(square[:, :, :], tables[:, bass.ds(g, 1), :].broadcast_to([P, 8, 16]),
                                        t["sel8"][:, :].unsqueeze(2).broadcast_to([P, 8, 16]), ALU.mult).then_inc(hot_done, 1)
                        dve.wait_ge(hot_done, g + 1)
                        dve.wait_ge(rowed, g + 1)
                        V.tensor_tensor(picked[:, :], row_ps[:, :], hot[0][:, :], ALU.mult).then_inc(picked_done, 1)
                        dve.wait_ge(summed, g + 1)
                        V.tensor_scalar(t["w_high"][:, :, bass.ds(o * P + 8 * j, 8)],
                                        sum_ps[:, 0:64].rearrange("p (i c) -> p i c", i=ND), 1.0, None, ALU.mult).then_inc(stored, 1)

        @block.tensor
        def _(pe):
            go = pe.value_load(flag[0:1, 0:1])
            with pe.If(go != 0):
                pe.wait_ge(ready, 1)
                with pe.Fori(0, ND) as o:
                    for j in range(16):
                        g = o * 16 + j
                        pe.wait_ge(stored, g + 1)
                        for i in range(2):
                            for half in range(2):
                                last = nc.tensor.matmul(rep[i][:, 512 * half:512 * half + 512], repeat[:, P * j:P * j + P],
                                                        codes[i][:, bass.ds(o * DIM + 512 * half, 512)], start=True, stop=True)
                        last.then_inc(repeated, 1)
                        pe.wait_ge(hot_done, g + 1)
                        for half in range(2):
                            last = nc.tensor.matmul(row_ps[:, 512 * half:512 * half + 512], square[:, :, :].rearrange("p a b -> p (a b)"),
                                                    hot[1][:, 512 * half:512 * half + 512], start=True, stop=True)
                        last.then_inc(rowed, 1)
                        pe.wait_ge(picked_done, g + 1)
                        for i in range(ND):
                            last = nc.tensor.matmul(sum_ps[:, 8 * i:8 * i + 8], picked[:, P * i:P * i + P], t["sel8"][:, :],
                                                    start=True, stop=True)
                        last.then_inc(summed, 1)


def general_rows(nc, t, flag, before, out):
    with ExitStack() as ctx:
        sb = lambda n, s, d=F32: ctx.enter_context(nc.sbuf_tensor(n, s, d))
        pb = lambda n, s: ctx.enter_context(nc.psum_tensor(n, s, F32))
        sem = lambda n: ctx.enter_context(nc.semaphore(n))
        h1 = sb("r_h1", [P, 2, DIM])
        low = sb("r_low", [P, 2, DIM])
        xn = sb("r_xn", [P, 2, DIM])
        x2_t = sb("r_x2_t", [P, ND, LEN])
        y_t = sb("r_y_t", [P, ND, LEN])
        stats = sb("r_stats", [P, 2, 2, 6])
        mv = sb("r_mv", [P, 2, 2])
        ve, ln, r0, sq, pr, co, rstd, mask, other = (sb(f"r_small{i}", [P, 2]) for i in range(9))
        xp = pb("r_xp", [P, 512])
        fp = pb("r_fp", [P, 512])
        op = pb("r_op", [P, 512])
        loaded, written = sem("r_loaded"), sem("r_written")
        dve_step, root, turned, taken, multiplied, y_done, back, added = (
            sem("r_dve_step"), sem("r_root"), sem("r_turned"), sem("r_taken"), sem("r_multiplied"), sem("r_y_done"),
            sem("r_back"), sem("r_added"))
        rows = (HEADS, TXT)
        cols = (slice(0, HEADS), slice(HEADS, LEN))
        DVE_STEPS = 15
        block = ctx.enter_context(nc.Block())

        def entry(ap, v, k):
            return ap[bass.ds(v, 1), cols[k], :].rearrange("a p l -> (a p) l")

        @block.sync
        def _(sp):
            go = sp.value_load(flag[0:1, 0:1])
            with sp.If(go != 0):
                def one(v):
                    wait(sp, written, v * 32)
                    for k in range(2):
                        sp.dma_start(h1[0:rows[k], k, :], entry(before, v, k)).then_inc(loaded, 16)
                        sp.dma_start(low[0:rows[k], k, :], entry(out, v, k)).then_inc(loaded, 16)
                    sp.wait_ge(dve_step, (v + 1) * DVE_STEPS)
                    for k in range(2):
                        sp.dma_start(entry(out, v, k), low[0:rows[k], k, :]).then_inc(written, 16)

                one(0)
                with sp.Fori(1, BATCH) as v:
                    one(v)
                sp.wait_ge(written, 32 * BATCH)

        @block.vector
        def _(dve):
            V = nc.vector
            go = dve.value_load(flag[0:1, 0:1])
            with dve.If(go != 0):
                V.memset(mv[:, :, :], 1.0).then_inc(added, 1)
                with dve.Fori(0, BATCH) as v:
                    done = [0]

                    def step(ins):
                        done[0] += 1
                        ins.then_inc(dve_step, 1)
                        dve.wait_ge(dve_step, v * DVE_STEPS + done[0])

                    dve.wait_ge(loaded, v * 64 + 64)
                    for k in range(2):
                        for i in range(2):
                            last = V.bn_stats(stats[0:rows[k], k, i, :], h1[0:rows[k], k, 512 * i:512 * i + 512])
                    step(last)
                    step(V.memset(ve[:, :], 1.0))
                    V.memset(ln[:, :], 1.0)
                    for k in range(2):
                        last = V.bn_aggr(mv[0:rows[k], k, :], stats[0:rows[k], k, :, :].rearrange("p a b -> p (a b)"))
                    step(last)
                    step(V.tensor_scalar(ve[:, :], mv[:, :, 1], EPS_LN, None, ALU.add))
                    dve.wait_ge(root, v * 2 + 2)
                    step(V.tensor_tensor(sq[:, :], r0[:, :], r0[:, :], ALU.mult))
                    step(V.tensor_tensor(pr[:, :], sq[:, :], ve[:, :], ALU.mult))
                    step(V.tensor_scalar(co[:, :], pr[:, :], -0.5, 1.5, ALU.mult, ALU.add))
                    step(V.tensor_tensor(rstd[:, :], co[:, :], r0[:, :], ALU.mult))
                    step(V.tensor_tensor(sq[:, :], rstd[:, :], rstd[:, :], ALU.mult))
                    step(V.tensor_tensor(pr[:, :], sq[:, :], mv[:, :, 1], ALU.mult))
                    step(V.tensor_scalar(mask[:, :], pr[:, :], float(DIM), NORM_LIMIT * NORM_LIMIT, ALU.mult, ALU.is_gt))
                    step(V.tensor_scalar(other[:, :], mask[:, :], -1.0, 1.0, ALU.mult, ALU.add))
                    for k in range(2):
                        last = V.tensor_scalar(xn[0:rows[k], k, :], h1[0:rows[k], k, :], mv[0:rows[k], k, 0:1],
                                               rstd[0:rows[k], k:k + 1], ALU.subtract, ALU.mult)
                    step(last)
                    for k in range(2):
                        last = V.tensor_scalar(low[0:rows[k], k, :], low[0:rows[k], k, :], other[0:rows[k], k:k + 1], None, ALU.mult)
                    step(last)
                    for r in range(4):
                        dve.wait_ge(turned, v * 4 + r + 1)
                        V.tensor_scalar(x2_t[:, 2 * r:2 * r + 2, :], xp[:, 0:2 * LEN].rearrange("p (j l) -> p j l", j=2),
                                        1.0, None, ALU.mult).then_inc(taken, 1)
                    for r in range(4):
                        side, k = r // 2, r % 2
                        part = slice(512 * side, 512 * side + 512)
                        dve.wait_ge(back, v * 4 + r + 1)
                        V.tensor_tensor(h1[0:rows[k], k, part], h1[0:rows[k], k, part], op[0:rows[k], :], ALU.add).then_inc(added, 1)
                        if r == 3:
                            dve.wait_ge(added, v * 4 + 5)
                    for k in range(2):
                        last = V.scalar_tensor_tensor(low[0:rows[k], k, :], h1[0:rows[k], k, :], mask[0:rows[k], k:k + 1],
                                                      low[0:rows[k], k, :], ALU.mult, ALU.add)
                    step(last)
                    assert done[0] == DVE_STEPS, done

        @block.scalar
        def _(act):
            A = nc.scalar
            go = act.value_load(flag[0:1, 0:1])
            with act.If(go != 0):
                with act.Fori(0, BATCH) as v:
                    act.wait_ge(dve_step, v * DVE_STEPS + 4)
                    A.activation(ln[:, :], ve[:, :], ACT.Ln).then_inc(root, 1)
                    act.wait_ge(root, v * 2 + 1)
                    A.activation(r0[:, :], ln[:, :], ACT.Exp, scale=-0.5).then_inc(root, 1)
                    for o in range(ND):
                        act.wait_ge(multiplied, v * ND + o + 1)
                        A.activation(y_t[:, o, :], fp[:, 0:LEN], ACT.Identity, bias=t["y_bias"][:, o:o + 1]).then_inc(y_done, 1)

        @block.tensor
        def _(pe):
            ident = t["ident"]
            go = pe.value_load(flag[0:1, 0:1])
            with pe.If(go != 0):
                with pe.Fori(0, BATCH) as v:
                    pe.wait_ge(dve_step, v * DVE_STEPS + DVE_STEPS - 1)
                    for r in range(4):
                        if r:
                            pe.wait_ge(taken, v * 4 + r)
                        for j in range(2):
                            for k in range(2):
                                last = nc.tensor.transpose(xp[:, LEN * j + cols[k].start:LEN * j + cols[k].stop],
                                                           xn[0:rows[k], k, P * (2 * r + j):P * (2 * r + j) + P],
                                                           ident[0:rows[k], 0:rows[k]])
                        last.then_inc(turned, 1)
                    pe.wait_ge(taken, v * 4 + 4)
                    for o in range(ND):
                        if o:
                            pe.wait_ge(y_done, v * ND + o)
                        for i in range(ND):
                            last = nc.tensor.matmul(fp[:, 0:LEN], t["w_high"][:, i, P * o:P * o + P], x2_t[:, i, :],
                                                    start=(i == 0), stop=(i == ND - 1))
                        last.then_inc(multiplied, 1)
                    pe.wait_ge(y_done, v * ND + ND)
                    for r in range(4):
                        side, k = r // 2, r % 2
                        if r:
                            pe.wait_ge(added, v * 4 + r + 1)
                        for j in range(4):
                            last = nc.tensor.transpose(op[0:rows[k], P * j:P * j + P], y_t[:, 4 * side + j, cols[k]], ident[:, :])
                        last.then_inc(back, 1)


def persistent(nc, ctx):
    t = {}
    for name, shape, dtype in (
            ("ident", [P, P], F32), ("sel8", [P, 8], F32), ("code_col", [P, 1], F32),
           
            ("a_neg", [P, ND, NS], F32), ("d_col", [P, ND], F32), ("dt_bias", [P, ND], F32), ("y_bias", [P, ND], F32),
            ("xpw_t", [P, ND, 2 * RANK], F32), ("dtw_t", [RANK, DIM], F32), ("mv1", [P, 2, 2], F32), ("mv2", [P, 2, 2], F32),
            ("over", [P, 2], F32), ("flag", [1, 1], I32)):
        t[name] = ctx.enter_context(nc.sbuf_tensor(name, shape, dtype))
    return t


def build(nc, dram, out):
    mixed = nc.dram_tensor("mixed", (BATCH, HEADS, LK), F32, kind="Internal").ap()
    before = nc.dram_tensor("before", (BATCH, LEN, DIM), F32, kind="Internal").ap()
    rows_bc = nc.dram_tensor("rows_bc", (2, 2 * NS, LEN), F32, kind="Internal").ap()
    kept = {"spread": nc.dram_tensor("spread_kept", (P, 16 * P), BF16, kind="Internal").ap()}
    with ExitStack() as ctx:
        t = persistent(nc, ctx)
        with ExitStack() as early:
            t["ramp"] = early.enter_context(nc.sbuf_tensor("ramp", [P, HALF], F32))
            constants(nc, t, dram, kept)
            token_mixer(nc, t, dram, mixed)
        with ExitStack() as low:
            t["w_low"] = low.enter_context(nc.sbuf_tensor("w_low", [P, ND, DIM], F32))
            dense_weights(nc, t, dram)
            scan_pass(nc, t, dram, mixed, before, rows_bc, out)
        general_path(nc, t, dram, kept, before, out)


_NAMES = {"x": "x", "txt": "txt", "L0_tok_log_dt": "log_dt", "L0_tok_Lambda": "Lambda",
          "L0_attn_A_log": "A_log", "L0_attn_D": "D", "L0_attn_x_proj_w": "x_proj_w",
          "L0_attn_dt_proj_w": "dt_proj_w", "L0_attn_dt_proj_b": "dt_proj_b",
          "L0_ffn_qweight": "qweight", "L0_ffn_lut4": "lut4", "L0_ffn_lut8": "lut8", "L0_ffn_bias": "bias"}


def kernel(**inputs):
    import numpy as _np
    import concourse.bacc as _bacc
    from concourse import mybir as _mybir
    from concourse.bass_utils import run_bass_kernel_spmd as _run

    nc = _bacc.Bacc("TRN2", target_bir_lowering=False, num_devices=1)
    arrays, dram = {}, {}
    for name, short in _NAMES.items():
        a = _np.ascontiguousarray(inputs[name])
        arrays[f"in_{name}"] = a
        dram[short] = nc.dram_tensor(f"in_{name}", a.shape, _mybir.dt.from_np(a.dtype), kind="ExternalInput").ap()
    out = nc.dram_tensor("out_0", (BATCH, LEN, DIM), _mybir.dt.float32, kind="ExternalOutput").ap()
    build(nc, dram, out)
    r = _run(nc, [arrays], core_ids=[0])
    return r.results[0]["out_0"]
```
